# Optimizing a Trainium2 kernel written in Bass

```python
import numpy as np
import jax
import jax.numpy as jnp

def _softmax(x, axis=-1):
    return jax.nn.softmax(x, axis=axis)

def _gelu(x):
    return jax.nn.gelu(x, approximate=True)

def _silu(x):
    return jax.nn.silu(x)

def _sigmoid(x):
    return jax.nn.sigmoid(x)

def _layernorm(x, axis=-1, eps=1e-05):
    m = jnp.mean(x, axis=axis, keepdims=True)
    v = jnp.var(x, axis=axis, keepdims=True)
    return (x - m) / jnp.sqrt(v + eps)

def _scatter_add(tgt, idx, src, axis=0):
    return tgt.at[idx].add(src)

def _segment_sum(src, seg, n):
    return jax.ops.segment_sum(src, seg, n)
kernel_name = 'mk_adaln_d1_jaxref_r8_dc5eee'

def setup_inputs(seed: int=0):
    np.random.seed(seed)
    _w = jnp.asarray

    def _L0_attn_setup():
        import jax, jax.numpy as jnp
        import numpy as np
        B, S, H_DIM = (2, 256, 256)
        N_HEADS, D_HEAD = (16, 128)
        key = jax.random.key(seed)
        k1, k2, k3 = jax.random.split(key, 3)
        x = jax.random.normal(k1, (B, S, H_DIM), dtype=jnp.float32)
        w_qkv = jax.random.normal(k2, (H_DIM, 3 * N_HEADS * D_HEAD), dtype=jnp.float32) * 0.02
        w_o = jax.random.normal(k3, (N_HEADS * D_HEAD, H_DIM), dtype=jnp.float32) * 0.02
        return {'x': x, 'w_qkv': w_qkv, 'w_o': w_o}
    _L0_attn_in = _L0_attn_setup()

    def _L0_ffn_setup():
        import jax, jax.numpy as jnp
        import numpy as np
        B, L, D = (2, 128, 256)
        E, K = (8, 2)
        H, HS = (176, 352)
        key = jax.random.key(seed)
        ks = jax.random.split(key, 9)
        s = 0.02
        return {'x': jax.random.normal(ks[0], (B, L, D), dtype=jnp.float32), 'gate_w': jax.random.normal(ks[1], (E, D), dtype=jnp.float32) * s, 'w_gate': jax.random.normal(ks[2], (E, D, H), dtype=jnp.float32) * s, 'w_up': jax.random.normal(ks[3], (E, D, H), dtype=jnp.float32) * s, 'w_down': jax.random.normal(ks[4], (E, H, D), dtype=jnp.float32) * s, 'shgate_w': jax.random.normal(ks[5], (D,), dtype=jnp.float32) * s, 'shw_gate': jax.random.normal(ks[6], (D, HS), dtype=jnp.float32) * s, 'shw_up': jax.random.normal(ks[7], (D, HS), dtype=jnp.float32) * s, 'shw_down': jax.random.normal(ks[8], (HS, D), dtype=jnp.float32) * s}
    _L0_ffn_in = _L0_ffn_setup()
    _L0_c = _w((lambda *s: np.random.randn(*s).astype(np.float32) * 0.05)(8, 256))
    _L0_wmod = _w((lambda *s: np.random.randn(*s).astype(np.float32) * 0.05)(256, 6 * 256) * 256 ** (-0.5))
    _d = {'L0_attn_x': _L0_attn_in['x'], 'L0_attn_w_qkv': _L0_attn_in['w_qkv'], 'L0_attn_w_o': _L0_attn_in['w_o'], 'L0_ffn_gate_w': _L0_ffn_in['gate_w'], 'L0_ffn_w_gate': _L0_ffn_in['w_gate'], 'L0_ffn_w_up': _L0_ffn_in['w_up'], 'L0_ffn_w_down': _L0_ffn_in['w_down'], 'L0_ffn_shgate_w': _L0_ffn_in['shgate_w'], 'L0_ffn_shw_gate': _L0_ffn_in['shw_gate'], 'L0_ffn_shw_up': _L0_ffn_in['shw_up'], 'L0_ffn_shw_down': _L0_ffn_in['shw_down'], 'L0_c': _L0_c, 'L0_wmod': _L0_wmod}
    _x0 = _d['L0_attn_x']
    _d['L0_attn_x'] = jax.random.normal(jax.random.fold_in(jax.random.key(seed), 1), (8, 256, 256), dtype=_x0.dtype)
    del _x0
    return _d

def reference(L0_attn_x, L0_attn_w_qkv, L0_attn_w_o, L0_ffn_gate_w, L0_ffn_w_gate, L0_ffn_w_up, L0_ffn_w_down, L0_ffn_shgate_w, L0_ffn_shw_gate, L0_ffn_shw_up, L0_ffn_shw_down, L0_c, L0_wmod):

    def _L0_attn_ref(x, w_qkv, w_o):
        import jax, jax.numpy as jnp
        import numpy as np
        B, S, H_DIM = (2, 256, 256)
        N_HEADS, D_HEAD = (16, 128)
        b, s, _ = x.shape
        qkv = jnp.einsum('bsh,hf->bsf', x, w_qkv)
        qkv = qkv.reshape(b, s, 3, N_HEADS, D_HEAD)
        q, k, v = (qkv[:, :, 0], qkv[:, :, 1], qkv[:, :, 2])
        q = q.transpose(0, 2, 1, 3)
        k = k.transpose(0, 2, 1, 3)
        v = v.transpose(0, 2, 1, 3)
        scores = jnp.einsum('bhqd,bhkd->bhqk', q, k) / jnp.sqrt(jnp.float32(D_HEAD))
        probs = jax.nn.softmax(scores, axis=-1)
        values = jnp.einsum('bhqk,bhkd->bhkd', probs, v)
        values = values.transpose(0, 2, 1, 3).reshape(b, s, N_HEADS * D_HEAD)
        out = jnp.einsum('bsf,fh->bsh', values, w_o)
        return out

    def _L0_ffn_ref(x, gate_w, w_gate, w_up, w_down, shgate_w, shw_gate, shw_up, shw_down):
        import jax, jax.numpy as jnp
        import numpy as np
        B, L, D = (2, 128, 256)
        E, K = (8, 2)
        H, HS = (176, 352)
        b, l, d = x.shape
        xf = x.reshape(-1, d)
        logits = jnp.einsum('td,ed->te', xf.astype(jnp.float32), gate_w)
        probs = jax.nn.softmax(logits.astype(jnp.float32), axis=-1)
        weights, indices = jax.lax.top_k(probs, K)
        weights = (weights / weights.sum(-1, keepdims=True)).astype(x.dtype)
        onehot = jax.nn.one_hot(indices, E, dtype=x.dtype)
        combine = jnp.einsum('tk,tke->te', weights, onehot)
        g = jnp.einsum('td,edh->teh', xf, w_gate)
        u = jnp.einsum('td,edh->teh', xf, w_up)
        h = jax.nn.silu(g) * u
        out = jnp.einsum('teh,ehd,te->td', h.astype(jnp.float32), w_down.astype(jnp.float32), combine.astype(jnp.float32))
        sgate = jax.nn.sigmoid(xf @ shgate_w)[:, None]
        sh = jax.nn.silu(xf @ shw_gate) * (xf @ shw_up) @ shw_down
        out = out + (sgate * sh).astype(jnp.float32)
        return out.astype(x.dtype).reshape(b, l, d)
    x = L0_attn_x
    mod = (_silu(L0_c) @ L0_wmod).reshape(L0_c.shape[0], 6, 1, -1)
    sa, ca, ga, sb, cb, gb = (mod[:, 0], mod[:, 1], mod[:, 2], mod[:, 3], mod[:, 4], mod[:, 5])
    ga = (2 * (ga >= 0) - 1) * jnp.maximum(jnp.abs(ga), 0.25)
    gb = (2 * (gb >= 0) - 1) * jnp.maximum(jnp.abs(gb), 0.25)
    h = _layernorm(x, axis=-1) * (1 + ca) + sa
    x = x + ga * _L0_attn_ref(h, L0_attn_w_qkv, L0_attn_w_o)
    h = _layernorm(x, axis=-1) * (1 + cb) + sb
    x = x + gb * _L0_ffn_ref(h, L0_ffn_gate_w, L0_ffn_w_gate, L0_ffn_w_up, L0_ffn_w_down, L0_ffn_shgate_w, L0_ffn_shw_gate, L0_ffn_shw_up, L0_ffn_shw_down)
    return x

_drawn_inputs = setup_inputs


def setup_inputs(seed=0):
    import zlib

    import numpy as np

    out = dict(_drawn_inputs(seed))
    spreads = {}
    factors = {'L0_ffn_gate_w': 8.0,
     'L0_ffn_w_gate': 8.0,
     'L0_ffn_w_up': 8.0,
     'L0_ffn_w_down': 8.0,
     'L0_ffn_shgate_w': 8.0,
     'L0_ffn_shw_gate': 8.0,
     'L0_ffn_shw_up': 8.0,
     'L0_ffn_shw_down': 8.0}
    for name, (base, spread) in spreads.items():
        noise = np.random.default_rng([zlib.crc32(name.encode()), seed]).standard_normal(out[name].shape)
        drawn = base * np.exp(spread * noise) if base else spread * noise
        out[name] = jnp.asarray(drawn.astype(out[name].dtype))
    for name, factor in factors.items():
        out[name] = (out[name] * factor).astype(out[name].dtype)
    return out
```

```python
from contextlib import ExitStack

import concourse.bass as bass
from concourse import mybir

P = 128
ALU = mybir.AluOpType
ACT = mybir.ActivationFunctionType
F32 = mybir.dt.float32
I32 = mybir.dt.int32
F32R = mybir.dt.float32r
AX_X = mybir.AxisListType.X
LN_EPS = 1e-5
NEWTON = 3
LN_LINKS = 5 + 3 * NEWTON
GATE_MIN = 0.25
SA, CA, GA, SB, CB, GB = range(6)


def adaln_block(nc, x, w_qkv, w_o, gate_w, w_gate, w_up, w_down, shgate_w, shw_gate, shw_up,
                shw_down, cond, wmod, ident_in, spread_in, order_in, out):
    B, S, D = x.shape
    HD = w_o.shape[0]
    DH = P
    NH = HD // DH
    DC = D // P
    TT = S // P
    E, _, H = w_gate.shape
    HS = shw_gate.shape[1]
    NF = E * H + HS
    FT = -(-NF // P)
    FE = E * H // P
    NT = 512
    TILES = B * S // NT
    TPT = NT // P
    BPT = NT // S
    SCALE = float(DH) ** -0.5
    G = E + 1
    GP = G + G % 2
    UNITS = B * NH
    SLOTS = 4
    assert DC == 2 and TT == 2 and S == 256 and NH % 2 == 0 and FE * P == E * H
    rows_of = [min(P, NF - j * P) for j in range(FT)]

    ctx = ExitStack()
    with ctx:
        keep, early, late = ctx.enter_context(ExitStack()), ExitStack(), ExitStack()

        def sb(where, name, shape, dt=F32):
            return where.enter_context(nc.sbuf_tensor(name, shape, dt))

        def sem(name):
            return ctx.enter_context(nc.semaphore(name))

        ident = sb(keep, "ident", [P, P])
        mod = sb(keep, "mod", [P, 6, DC, B + 1])
        x1 = sb(keep, "x1", [P, B * TT, D])
        wraw = sb(keep, "wraw", [P, SLOTS, 4 * D])
        wq_hi = sb(early, "wq_hi", [P, NH, 3, DC, DH], F32R)
        wq_lo = sb(early, "wq_lo", [P, NH, 3, DC, DH], F32R)
        wo_hi = sb(early, "wo_hi", [P, NH, D], F32R)
        wo_lo = sb(early, "wo_lo", [P, NH, D], F32R)
        qk_hi = sb(early, "qk_hi", [P, 2, 2, S], F32R)
        qk_lo = sb(early, "qk_lo", [P, 2, 2, S], F32R)
        h_hi = sb(early, "h_hi", [P, DC, 2 * S], F32R)
        h_lo = sb(early, "h_lo", [P, DC, 2 * S], F32R)
        h_next = sb(early, "h_next", [P, DC, S])
        x_ln = sb(early, "x_ln", [P, TT, D])
        xn = sb(early, "xn", [P, TT, D])
        x_res = sb(early, "x_res", [P, TT, D])
        probs = sb(early, "probs", [P, 2, TT, S])
        psum_half = sb(early, "psum_half", [P, 2, S])
        psum = sb(early, "psum", [P, 2, S])
        psum_hi = sb(early, "psum_hi", [P, 2, S], F32R)
        psum_lo = sb(early, "psum_lo", [P, 2, S], F32R)
        ones = sb(early, "ones", [P, P], F32R)
        qsum = sb(early, "qsum", [P, 2, S])
        vals = sb(early, "vals", [P, 2, S])
        o_hi = sb(early, "o_hi", [P, 2, S], F32R)
        o_lo = sb(early, "o_lo", [P, 2, S], F32R)
        yT = sb(early, "yT", [P, DC, S])
        stats = sb(early, "stats", [P, TT, 6])
        mv = sb(early, "mv", [P, TT, 2])
        rstd = sb(early, "rstd", [P, TT])
        rtmp = sb(early, "rtmp", [P, TT])
        smax = sb(early, "smax", [P, 2, TT])
        nmax = sb(early, "nmax", [P, 2, TT])
        rsum = sb(early, "rsum", [P, 2, TT])
        rinv = sb(early, "rinv", [P, 2, TT])
        early.close()
        wmod_sb = x1[:].rearrange("p a b -> p (a b)")[:, 0:DC * 6 * D].rearrange("p (c n) -> p c n", c=DC)
        c_sb = wraw[0:B, SLOTS - 1, 0:D]
        cT = wraw[:, SLOTS - 1, D:D + DC * B].rearrange("p (c b) -> p c b", c=DC)
        cTs = wraw[:, SLOTS - 1, 2 * D:2 * D + DC * B].rearrange("p (c b) -> p c b", c=DC)
        mtmp = wraw[:, SLOTS - 1, 3 * D:3 * D + 2 * DC * B].rearrange("p (a c b) -> p a c b", a=2, c=DC)
        raws = ExitStack()
        graw = sb(raws, "graw", [P, DC, NF])
        uraw = sb(raws, "uraw", [P, DC, NF])
        raws.close()
        g_lo = sb(late, "g_lo", [P, DC, NF], F32R)
        u_lo = sb(late, "u_lo", [P, DC, NF], F32R)
        g_hi = sb(late, "g_hi", [P, DC, NF], F32R)
        u_hi = sb(late, "u_hi", [P, DC, NF], F32R)
        d_hi = sb(late, "d_hi", [P, FT, D], F32R)
        d_lo = sb(late, "d_lo", [P, FT, D], F32R)
        h2_hi = sb(late, "h2_hi", [P, DC, B * S], F32R)
        h2_lo = sb(late, "h2_lo", [P, DC, B * S], F32R)
        h2 = sb(late, "h2", [P, DC, NT])
        xn2 = sb(late, "xn2", [P, TPT, D])
        f_hi = sb(late, "f_hi", [P, 2, NT], F32R)
        f_lo = sb(late, "f_lo", [P, 2, NT], F32R)
        fs = sb(late, "fs", [P, NT])
        fu = sb(late, "fu", [P, 2, NT])
        gw_hi = sb(late, "gw_hi", [P, DC, GP], F32R)
        gw_lo = sb(late, "gw_lo", [P, DC, GP], F32R)
        combT = sb(late, "combT", [2 * G, B * S], F32R)
        spread = sb(late, "spread", [2 * G, FT * P], F32R)
        late_small = sb(late, "late_small", [P, 1024])
        sb_combr = sb(late, "comb_r", [P, TPT, G], F32R)
        y2T = h2
        x2 = xn2
        late.close()
        draw = wraw[:].rearrange("p a b -> p (a b)")[:, 0:FT * D].rearrange("p (j d) -> p j d", j=FT)
        spread_raw = fs[0:2 * G, :]
        gw_sb = late_small[0:G, 0:D]
        gwT = late_small[:, D:D + DC * GP].rearrange("p (c g) -> p c g", c=DC)
        off = [D + 32]

        def small(n):
            a = off[0]
            off[0] += n
            return late_small[:, a:a + n]

        order = small(TPT * E).rearrange("p (t e) -> p t e", t=TPT)
        lg = small(TPT * GP).rearrange("p (t e) -> p t e", t=TPT)
        pe_ = small(TPT * GP).rearrange("p (t e) -> p t e", t=TPT)
        pr = small(TPT * E).rearrange("p (t e) -> p t e", t=TPT)
        sel1 = small(TPT * E).rearrange("p (t e) -> p t e", t=TPT)
        sel2 = small(TPT * E).rearrange("p (t e) -> p t e", t=TPT)
        tmp8 = small(TPT * E).rearrange("p (t e) -> p t e", t=TPT)
        comb = small(TPT * G).rearrange("p (t e) -> p t e", t=TPT)
        comb2 = small(TPT * 2 * G).rearrange("p (t e) -> p t e", t=TPT)
        comb_r = sb_combr[:]
        m1, m2, kk, rr = (small(TPT) for _ in range(4))
        stats2 = small(TPT * 6).rearrange("p (t e) -> p t e", t=TPT)
        mv2 = small(TPT * 2).rearrange("p (t e) -> p t e", t=TPT)
        rstd2 = small(TPT)
        rtmp2 = small(TPT)
        assert off[0] <= 1024

        bank = [ctx.enter_context(nc.psum_tensor(f"bank{i}", [P, 512], F32)) for i in range(8)]
        qk_ps = [bank[i][:].rearrange("p (a s) -> p a s", a=2) for i in (0, 1)]
        s_ps = [bank[i][:].rearrange("p (t s) -> p t s", t=TT) for i in (2, 3)]
        v_ps = [bank[i][:].rearrange("p (a s) -> p a s", a=2) for i in (4, 5)]
        acc = bank[6][:].rearrange("p (c s) -> p c s", c=DC)
        tr = bank[7][:].rearrange("p (c s) -> p c s", c=2)

        cst_in = sem("cst_in")
        wmod_in = [sem(f"wmod_in{i}") for i in range(2)]
        c_tr = sem("c_tr")
        c_copied = sem("c_copied")
        c_silu = sem("c_silu")
        mod_made = sem("mod_made")
        mod_chain = sem("mod_chain")
        mod_ready = sem("mod_ready")
        x_in = sem("x_in")
        xres_in = sem("xres_in")
        w_in = [sem(f"w_in{i}") for i in range(SLOTS)]
        w_hi_done = sem("w_hi_done")
        w_lo_done = sem("w_lo_done")
        ln_chain = sem("ln_chain")
        xn_done = sem("xn_done")
        xn_tr = sem("xn_tr")
        hn_done = sem("hn_done")
        h_hi_done = sem("h_hi_done")
        h_lo_done = sem("h_lo_done")
        qk_made = sem("qk_made")
        qk_hi_done = sem("qk_hi_done")
        qk_lo_done = sem("qk_lo_done")
        v_made = sem("v_made")
        s_made = sem("s_made")
        smax_done = sem("smax_done")
        nmax_done = sem("nmax_done")
        exp_done = sem("exp_done")
        rinv_done = sem("rinv_done")
        half_done = sem("half_done")
        psum_done = sem("psum_done")
        psum_hi_done = sem("psum_hi_done")
        psum_lo_done = sem("psum_lo_done")
        ones_done = sem("ones_done")
        qsum_done = sem("qsum_done")
        vals_done = sem("vals_done")
        o_hi_done = sem("o_hi_done")
        o_lo_done = sem("o_lo_done")
        wo_done = sem("wo_done")
        y_done = sem("y_done")
        y_tr = sem("y_tr")
        x1_done = sem("x1_done")
        fw_in = sem("fw_in")
        dw_in = sem("dw_in")
        small_in = sem("small_in")
        rank_in = sem("rank_in")
        piece_in = sem("piece_in")
        spread_done = sem("spread_done")
        gw_tr = sem("gw_tr")
        gw_done = sem("gw_done")
        gu_hi_done = sem("gu_hi_done")
        gu_lo_done = sem("gu_lo_done")
        d_hi_done = sem("d_hi_done")
        d_lo_done = sem("d_lo_done")
        ln2_chain = sem("ln2_chain")
        xn2_done = sem("xn2_done")
        xn2_tr = sem("xn2_tr")
        h2_done = sem("h2_done")
        h2_hi_done = sem("h2_hi_done")
        h2_lo_done = sem("h2_lo_done")
        lg_made = sem("lg_made")
        gate_chain = sem("gate_chain")
        gate_sub = sem("gate_sub")
        gate_exp = sem("gate_exp")
        comb_done = sem("comb_done")
        comb_tr = sem("comb_tr")
        combT_done = sem("combT_done")
        g_made = sem("g_made")
        u_made = sem("u_made")
        c_made = sem("c_made")
        silu_done = sem("silu_done")
        fu_done = sem("fu_done")
        fc_done = sem("fc_done")
        f_hi_done = sem("f_hi_done")
        f_lo_done = sem("f_lo_done")
        d_made = sem("d_made")
        y2_done = sem("y2_done")
        y2_tr = sem("y2_tr")
        x2_done = sem("x2_done")
        out_done = sem("out_done")

        def f32(ap):
            return ap.bitcast(F32)

        x_v = x.rearrange("b (t p) d -> b p t d", p=P)
        out_v = out.rearrange("b (t p) d -> p (b t) d", p=P)
        wqkv_v = w_qkv.rearrange("(c p) (a h d) -> h p a c d", p=P, a=3, h=NH)
        wo_v = w_o.rearrange("(h p) n -> h p n", p=P)
        MODS = 6 * DC

        STEP_Y, STEP_YT, STEP_X1, STEP_LN, STEP_XT, STEP_HN = 3, 5, 6, 7, 10, 11

        block = ctx.enter_context(nc.Block())

        @block.sync
        def _(sp):
            sp.dma_start(ident[:], ident_in).then_inc(cst_in, 16)
            sp.dma_start(c_sb, cond).then_inc(cst_in, 16)
            wmod_v = wmod.rearrange("(c p) n -> p c n", p=P)
            sp.dma_start(wmod_sb[:, :, 0:2 * D], wmod_v[:, :, 0:2 * D]).then_inc(wmod_in[0], 16)
            sp.dma_start(x_ln[:], x_v[0]).then_inc(x_in, 16)

            def head_weights(h):
                if h >= SLOTS:
                    sp.wait_ge(w_lo_done, h - SLOTS + 1)
                if h == SLOTS - 1:
                    sp.wait_ge(mod_ready, 1)
                slot = wraw[:, h % SLOTS, :]
                dst = slot[:, 0:3 * D].rearrange("p (a c d) -> p a c d", a=3, c=DC)
                for a in range(3):
                    sp.dma_start(dst[:, a], wqkv_v[h][:, a]).then_inc(w_in[h % SLOTS], 16)
                sp.dma_start(slot[:, 3 * D:4 * D], wo_v[h]).then_inc(w_in[h % SLOTS], 16)

            head_weights(0)
            head_weights(1)
            sp.dma_start(wmod_sb[:, :, 2 * D:6 * D], wmod_v[:, :, 2 * D:6 * D]).then_inc(wmod_in[1], 16)
            sp.dma_start(x_res[:], x_v[0]).then_inc(xres_in, 16)
            for h in range(2, NH):
                head_weights(h)
                if h == SLOTS:
                    sp.wait_ge(xn_done, 1)
                    sp.dma_start(x_ln[:], x_v[1]).then_inc(x_in, 16)
            sp.wait_ge(w_lo_done, NH)
            sp.dma_start(draw[:, 0:FE, :], w_down.rearrange("e h d -> (e h) d").rearrange(
                "(j p) d -> p j d", p=P)).then_inc(dw_in, 16)
            full = HS // P
            sp.dma_start(draw[:, FE:FE + full, :], shw_down[0:full * P, :].rearrange(
                "(j p) d -> p j d", p=P)).then_inc(dw_in, 16)
            sp.dma_start(draw[0:HS - full * P, FE + full, :], shw_down[full * P:HS, :]).then_inc(dw_in, 16)
            with sp.Fori(1, B - 1) as b:
                sp.wait_ge(x1_done, b)
                sp.dma_start(x_res[:], x_v[b]).then_inc(xres_in, 16)
                sp.wait_ge(xn_done, b + 1)
                sp.dma_start(x_ln[:], x_v[b + 1]).then_inc(x_in, 16)
            sp.wait_ge(x1_done, B - 1)
            sp.dma_start(x_res[:], x_v[B - 1]).then_inc(xres_in, 16)
            sp.wait_ge(xn_done, B)
            sp.dma_start(x_ln[:], x_v[B - 1]).then_inc(x_in, 16)

            sp.wait_ge(qk_made, UNITS)
            sp.wait_ge(v_made, UNITS)
            for raw, w, shw in ((graw, w_gate, shw_gate), (uraw, w_up, shw_up)):
                for c in range(DC):
                    sp.dma_start(raw[:, c, 0:E * H].rearrange("p (e h) -> p e h", e=E),
                                 w[:, c * P:(c + 1) * P, :].rearrange("e p h -> p e h")).then_inc(fw_in, 16)
                sp.dma_start(raw[:, :, E * H:NF], shw.rearrange("(c p) h -> p c h", p=P)).then_inc(fw_in, 16)
            sp.wait_ge(x1_done, B)
            sp.dma_start(gw_sb[0:E, :], gate_w).then_inc(small_in, 16)
            sp.dma_start(gw_sb[E:G, :], shgate_w.rearrange("(a d) -> a d", a=1)).then_inc(small_in, 16)
            sp.dma_start(order, order_in.rearrange("p (t e) -> p t e", t=TPT)).then_inc(rank_in, 16)
            for q in range(0, FT * P, NT):
                n = min(NT, FT * P - q)
                if q:
                    sp.wait_ge(spread_done, q // NT)
                sp.dma_start(spread_raw[:, 0:n], spread_in[:, q:q + n]).then_inc(piece_in, 16)
            with sp.Fori(0, TILES) as t:
                sp.wait_ge(x2_done, t + 1)
                sp.dma_start(out_v[:, bass.ds(t * TPT, TPT), :], x2[:]).then_inc(out_done, 16)
            sp.wait_ge(out_done, 16 * TILES)

        @block.tensor
        def _(pe):
            def three(dst, lhs, rhs, start, stop, skip=False):
                n = len(lhs)
                for k in range(n):
                    for m, (i, j) in enumerate(((0, 0), (1, 0), (0, 1))):
                        mm = nc.tensor.matmul(dst, lhs[k][i], rhs[k][j], start=start and k == 0 and m == 0,
                                              stop=stop and k == n - 1 and m == 2, skip_group_check=skip)
                return mm

            pe.wait_ge(cst_in, 32)
            for c in range(DC):
                mm = nc.tensor.transpose(bank[0][:, c * B:(c + 1) * B], c_sb[:, c * P:(c + 1) * P], ident[0:B, 0:B])
            mm.then_inc(c_tr, 1)
            pe.wait_ge(c_silu, 1)
            mps = bank[1][:, 0:MODS * B].rearrange("p (m b) -> p m b", m=MODS)
            for part, (a, z) in enumerate(((0, 2 * DC), (2 * DC, MODS))):
                pe.wait_ge(wmod_in[part], 16)
                for m in range(a, z):
                    for c in range(DC):
                        mm = nc.tensor.matmul(mps[:, m, :] if part == 0 else bank[5][:, m * B:(m + 1) * B],
                                              wmod_sb[:, c, m * P:(m + 1) * P], cTs[:, c, :],
                                              start=c == 0, stop=c == DC - 1)
                mm.then_inc(mod_made, 1)

            def x_transposes(b):
                pe.wait_ge(xn_done, b + 1)
                if not isinstance(b, int) or b >= 2:
                    pe.wait_ge(x1_done, b - 1)
                for c in range(DC):
                    for t in range(TT):
                        mm = nc.tensor.transpose(tr[:, c, t * P:(t + 1) * P], xn[:, t, c * P:(c + 1) * P], ident[:])
                mm.then_inc(xn_tr, 1)

            def y_transposes(b):
                pe.wait_ge(y_done, b + 1)
                pe.wait_ge(hn_done, min(b + 2, B) if isinstance(b, int) else b + 2)
                for t in range(TT):
                    for c in range(DC):
                        mm = nc.tensor.transpose(tr[:, t, c * P:(c + 1) * P], yT[:, c, t * P:(t + 1) * P], ident[:])
                mm.then_inc(y_tr, 1)

            def step(b, h):
                i = b * NH + h
                first = isinstance(b, int)
                new = not first or i < UNITS

                def has(lag):
                    return not first or 0 <= i - lag < UNITS

                def act_rows(lag):
                    bb = b if h >= lag else b - 1
                    q = bass.ds((bb % 2) * S, S)
                    return [(h_hi[:, c, q], h_lo[:, c, q]) for c in range(DC)]

                if new:
                    if first:
                        pe.wait_ge(w_lo_done, h + 1)
                    if h == 0:
                        pe.wait_ge(h_lo_done, b + 1)
                    if not first or i >= 2:
                        pe.wait_ge(qk_lo_done, i - 1)
                    for a in range(2):
                        mm = three(qk_ps[h % 2][:, a, :],
                                   [(wq_hi[:, h, a, c, :], wq_lo[:, h, a, c, :]) for c in range(DC)],
                                   act_rows(0), True, True)
                    mm.then_inc(qk_made, 1)
                if has(1):
                    r = (h - 1) % 2
                    pe.wait_ge(qk_lo_done, i)
                    if not first or i >= 3:
                        pe.wait_ge(exp_done, i - 2)
                    for t in range(TT):
                        q = slice(t * P, (t + 1) * P)
                        mm = three(s_ps[r][:, t, :], [(qk_hi[:, r, 0, q], qk_lo[:, r, 0, q])],
                                   [(qk_hi[:, r, 1, :], qk_lo[:, r, 1, :])], True, True)
                    mm.then_inc(s_made, 1)
                if has(3):
                    g = (h - 3) % NH
                    if g == 0 and (not first or b >= 1):
                        pe.wait_ge(y_done, b)
                    pe.wait_ge(o_lo_done, i - 2)
                    for c in range(DC):
                        f = slice(c * P, (c + 1) * P)
                        mm = three(acc[:, c, :], [(wo_hi[:, g, f], wo_lo[:, g, f])],
                                   [(o_hi[:, g % 2, :], o_lo[:, g % 2, :])], g == 0 and c == 0,
                                   g == NH - 1 and c == DC - 1, skip=True)
                    mm.then_inc(wo_done, 1)
                if has(2):
                    g, r = (h - 2) % NH, h % 2
                    if not first or i >= 4:
                        pe.wait_ge(vals_done, i - 3)
                    if first and i == 2:
                        pe.wait_ge(mod_ready, 1)
                        pe.wait_ge(ones_done, 1)
                    three(v_ps[r][:, 0, :], [(wq_hi[:, g, 2, c, :], wq_lo[:, g, 2, c, :]) for c in range(DC)],
                          act_rows(2), True, True)
                    pe.wait_ge(psum_lo_done, i - 1)
                    nc.tensor.matmul(v_ps[r][:, 1, :], ones[:], psum_hi[:, r, :], start=True, stop=False)
                    nc.tensor.matmul(v_ps[r][:, 1, :], ones[:], psum_lo[:, r, :], start=False,
                                     stop=True).then_inc(v_made, 1)
                if new and h == STEP_XT:
                    x_transposes(b + 1)
                if (not first or b >= 1) and h == STEP_YT:
                    y_transposes(b - 1)

            x_transposes(0)
            for h in range(NH):
                step(0, h)
            with pe.Fori(1, B) as b:
                for h in range(NH):
                    step(b, h)
            for h in range(STEP_YT + 1):
                step(B, h)

            tra, trb = (bank[i][:].rearrange("p (c s) -> p c s", c=2) for i in (5, 6))
            acc2 = [bank[3], bank[4]]

            pe.wait_ge(small_in, 32)
            pe.wait_ge(x1_done, B)
            for c in range(DC):
                mm = nc.tensor.transpose(bank[7][:, c * GP:c * GP + G], gw_sb[:, c * P:(c + 1) * P], ident[0:G, 0:G])
            mm.then_inc(gw_tr, 1)

            def rows_transposes(g):
                pe.wait_ge(xn2_done, g + 1)
                if g:
                    pe.wait_ge(h2_done, g)
                for c in range(DC):
                    for t in range(TPT):
                        mm = nc.tensor.transpose((bank[5], bank[6])[c][:, t * P:(t + 1) * P],
                                                 xn2[:, t, c * P:(c + 1) * P], ident[:])
                mm.then_inc(xn2_tr, 1)

            def logits(g):
                pe.wait_ge(h2_lo_done, g + 1)
                if g == 0:
                    pe.wait_ge(gw_done, 2)
                else:
                    pe.wait_ge(combT_done, g)
                for t in range(TPT):
                    q = slice((g * TPT + t) * P, (g * TPT + t + 1) * P)
                    mm = three(bank[7][:, t * GP:(t + 1) * GP],
                               [(h2_hi[:, c, q], h2_lo[:, c, q]) for c in range(DC)],
                               [(gw_hi[:, c, :], gw_lo[:, c, :]) for c in range(DC)], True, True)
                mm.then_inc(lg_made, 1)

            def comb_transposes(g):
                pe.wait_ge(comb_done, g + 1)
                for t in range(TPT):
                    mm = nc.tensor.transpose(bank[7][0:2 * G, t * P:(t + 1) * P], comb2[:, t, :], ident[:])
                mm.then_inc(comb_tr, 1)

            def features(t, j, first):
                i = t * FT + j
                n = rows_of[j]
                f = slice(j * P, j * P + n)
                rhs = [(h2_hi[:, c, bass.ds(t * NT, NT)], h2_lo[:, c, bass.ds(t * NT, NT)]) for c in range(DC)]
                if first:
                    pe.wait_ge(gu_lo_done, j + 1)
                if first and j == 0:
                    pe.wait_ge(h2_lo_done, 1)
                if not first or i:
                    pe.wait_ge(silu_done, i)
                three(bank[0][0:n, :], [(g_hi[:, c, f], g_lo[:, c, f]) for c in range(DC)], rhs,
                      True, True).then_inc(g_made, 1)
                if not first or i:
                    pe.wait_ge(fu_done, i)
                    pe.wait_ge(fc_done, i)
                if first and j == 0:
                    pe.wait_ge(combT_done, 1)
                    pe.wait_ge(spread_done, -(-FT * P // NT))
                three(bank[1][0:n, :], [(u_hi[:, c, f], u_lo[:, c, f]) for c in range(DC)], rhs,
                      True, True).then_inc(u_made, 1)
                nc.tensor.matmul(bank[2][0:n, :], spread[:, f], combT[:, bass.ds(t * NT, NT)],
                                 start=True, stop=True).then_inc(c_made, 1)

            def down(t, j, first, i):
                n = rows_of[j]
                if first or j == FT - 1:
                    pe.wait_ge(d_lo_done, j + 1)
                pe.wait_ge(f_lo_done, i + 1)
                if j == 0 and not (isinstance(t, int) and t == 0):
                    pe.wait_ge(y2_done, t)
                for c in range(DC):
                    q = slice(c * P, (c + 1) * P)
                    mm = three(acc2[c][:], [(d_hi[0:n, j, q], d_lo[0:n, j, q])],
                               [(f_hi[0:n, j % 2, :], f_lo[0:n, j % 2, :])], j == 0, j == FT - 1, skip=True)
                mm.then_inc(d_made, 1)

            def out_transposes(t):
                pe.wait_ge(y2_done, t + 1)
                if not (isinstance(t, int) and t == 0):
                    pe.wait_ge(x2_done, t)
                for k in range(TPT):
                    for c in range(DC):
                        mm = nc.tensor.transpose((tra, trb)[k // 2][:, k % 2, c * P:(c + 1) * P],
                                                 y2T[:, c, k * P:(k + 1) * P], ident[:])
                mm.then_inc(y2_tr, 1)

            rows_transposes(0)
            logits(0)
            comb_transposes(0)
            for j in range(FT):
                features(0, j, True)
                if j:
                    down(0, j - 1, True, j - 1)
                g, k = 1 + j // 4, j % 4
                if g < TILES:
                    if k == 0:
                        rows_transposes(g)
                    if k == 1:
                        logits(g)
                    if k == 3:
                        comb_transposes(g)
            with pe.Fori(1, TILES) as t:
                for j in range(FT):
                    features(t, j, False)
                    if j == 0:
                        down(t - 1, FT - 1, False, t * FT - 1)
                    else:
                        down(t, j - 1, False, t * FT + j - 1)
                    if j == 2:
                        out_transposes(t - 1)
            down(TILES - 1, FT - 1, False, TILES * FT - 1)
            out_transposes(TILES - 1)


        @block.scalar
        def _(act):
            act.wait_ge(c_tr, 1)
            nc.scalar.activation(cTs, bank[0][:, 0:DC * B].rearrange("p (c b) -> p c b", c=DC),
                                 ACT.Silu).then_inc(c_silu, 1)

            def copy(dst, src):
                return nc.scalar.activation(dst, src, ACT.Copy)

            def split_head(h):
                act.wait_ge(w_in[h % SLOTS], 64 * (h // SLOTS + 1))
                raw = wraw[:, h % SLOTS, :]
                copy(wq_hi[:, h].rearrange("p a c d -> p (a c d)"), raw[:, 0:3 * D])
                copy(wo_hi[:, h, :], raw[:, 3 * D:4 * D]).then_inc(w_hi_done, 1)

            def step(b, h):
                i = b * NH + h
                first = isinstance(b, int)
                new = not first or i < UNITS
                r3 = (h - 3) % 2

                def has(lag):
                    return not first or 0 <= i - lag < UNITS

                if first and b == 0 and h + 3 < NH:
                    split_head(h + 3)
                if has(3):
                    if not first or i >= 5:
                        act.wait_ge(vals_done, i - 4)
                    act.wait_ge(v_made, i - 2)
                    copy(qsum[:, r3, :], v_ps[r3][:, 1, :]).then_inc(qsum_done, 1)
                if new:
                    act.wait_ge(qk_made, i + 1)
                    if not first or i >= 2:
                        act.wait_ge(s_made, i - 1)
                    copy(qk_hi[:, h % 2], qk_ps[h % 2]).then_inc(qk_hi_done, 1)
                if has(1):
                    r = (h - 1) % 2
                    if not first or i >= 3:
                        act.wait_ge(psum_done, i - 2)
                    act.wait_ge(nmax_done, i)
                    for t in range(TT):
                        e = nc.scalar.activation(probs[:, r, t, :], s_ps[r][:, t, :], ACT.Exp,
                                                 bias=nmax[:, r, t:t + 1], scale=SCALE,
                                                 accum_out=rsum[:, r, t:t + 1])
                    e.then_inc(exp_done, 1)
                if has(3):
                    act.wait_ge(vals_done, i - 2)
                    if not first or i >= 5:
                        act.wait_ge(wo_done, i - 4)
                    copy(o_hi[:, r3 % 2, :], vals[:, r3 % 2, :]).then_inc(o_hi_done, 1)
                if has(1):
                    act.wait_ge(psum_done, i)
                    if not first or i >= 3:
                        act.wait_ge(v_made, i - 2)
                    copy(psum_hi[:, r, :], psum[:, r, :]).then_inc(psum_hi_done, 1)

            split_head(0)
            split_head(1)
            split_head(2)
            for h in range(NH):
                step(0, h)
            with act.Fori(1, B) as b:
                for h in range(NH):
                    step(b, h)
            for h in range(3):
                step(B, h)

            def split_down(j):
                n = rows_of[j]
                if j == 0:
                    act.wait_ge(dw_in, 48)
                copy(d_hi[0:n, j, :], draw[0:n, j, :]).then_inc(d_hi_done, 1)

            def split_features(j):
                f = slice(j * P, j * P + rows_of[j])
                if j == 0:
                    act.wait_ge(fw_in, 96)
                copy(g_hi[:, :, f], graw[:, :, f])
                copy(u_hi[:, :, f], uraw[:, :, f]).then_inc(gu_hi_done, 1)

            def rows2_hi(g):
                act.wait_ge(h2_done, g + 1)
                copy(h2_hi[:, :, g * NT:(g + 1) * NT], h2[:]).then_inc(h2_hi_done, 1)

            def gates_exp(g):
                act.wait_ge(gate_sub, g + 1)
                nc.scalar.activation(pe_[:, :, 0:G], pe_[:, :, 0:G], ACT.Exp).then_inc(gate_exp, 1)

            def comb_out(g):
                act.wait_ge(comb_tr, g + 1)
                copy(combT[:, g * NT:(g + 1) * NT], bank[7][0:2 * G, 0:NT]).then_inc(combT_done, 1)

            def product_hi(i, j, first):
                n = rows_of[j]
                act.wait_ge(fc_done, i + 1)
                if not first or i >= 2:
                    act.wait_ge(d_made, i - 1)
                r = j % 2
                copy(f_hi[0:n, j % 2, :], fu[0:n, r, :]).then_inc(f_hi_done, 1)

            def silu(i, j, first):
                n = rows_of[j]
                act.wait_ge(g_made, i + 1)
                if not first or i:
                    act.wait_ge(fu_done, i)
                nc.scalar.activation(fs[0:n, :], bank[0][0:n, :], ACT.Silu).then_inc(silu_done, 1)

            act.wait_ge(x1_done, B)
            pieces = -(-FT * P // NT)
            for k in range(pieces):
                act.wait_ge(piece_in, 16 * (k + 1))
                q, n = k * NT, min(NT, FT * P - k * NT)
                copy(spread[:, q:q + n], spread_raw[:, 0:n]).then_inc(spread_done, 1)
            split_features(0)
            split_down(0)
            rows2_hi(0)
            split_features(1)
            split_down(1)
            gates_exp(0)
            comb_out(0)
            for j in range(FT):
                if j:
                    product_hi(j - 1, j - 1, True)
                silu(j, j, True)
                if j + 2 < FT:
                    split_features(j + 2)
                    split_down(j + 2)
                g, k = 1 + j // 4, j % 4
                if g < TILES:
                    if k == 0:
                        rows2_hi(g)
                    if k == 1:
                        gates_exp(g)
                    if k == 3:
                        comb_out(g)
            with act.Fori(1, TILES) as t:
                for j in range(FT):
                    i = t * FT + j
                    product_hi(i - 1, (j - 1) % FT, False)
                    silu(i, j, False)
            product_hi(TILES * FT - 1, FT - 1, False)

        @block.vector
        def _(dve):
            def lo(dst, src, hi):
                return nc.vector.tensor_tensor(dst, src, f32(hi), ALU.subtract)

            chains = {}

            def link(s, ins):
                chains[s.name] = chains.get(s.name, 0) + 1
                ins.then_inc(s, 1)
                dve.wait_ge(s, chains[s.name])

            def counted(s, base):
                n = [0]

                def link(ins):
                    n[0] += 1
                    ins.then_inc(s, 1)
                    dve.wait_ge(s, base + n[0])

                return link

            def deviation(link, v, y, t):
                ts, stt = nc.vector.tensor_scalar, nc.vector.scalar_tensor_tensor
                link(ts(v, v, LN_EPS, None, ALU.add))
                link(ts(t.bitcast(I32), v.bitcast(I32), 1, None, ALU.arith_shift_right))
                link(ts(y.bitcast(I32), t.bitcast(I32), -1.0, float(0x5F3759DF), ALU.mult, ALU.add))
                for _ in range(NEWTON):
                    link(stt(t, y, -0.5, y, ALU.mult, ALU.mult))
                    link(nc.vector.tensor_tensor(t, t, v, ALU.mult))
                    link(stt(y, t, 1.5, y, ALU.add, ALU.mult))

            link(mod_chain, nc.vector.memset(mod[:], 0.0))

            def gate(k, src):
                sgn, mag = mtmp[:, 0], mtmp[:, 1]
                link(mod_chain, nc.vector.tensor_scalar(sgn, src, 0.0, 2.0, ALU.is_ge, ALU.mult))
                link(mod_chain, nc.vector.tensor_scalar(sgn, sgn, -1.0, None, ALU.add))
                link(mod_chain, nc.vector.tensor_tensor(mag, sgn, src, ALU.mult))
                link(mod_chain, nc.vector.tensor_scalar(mag, mag, GATE_MIN, None, ALU.max))
                link(mod_chain, nc.vector.tensor_tensor(mod[:, k, :, 0:B], sgn, mag, ALU.mult))

            dve.wait_ge(c_tr, 1)

            def normalise(b):
                link = counted(ln_chain, LN_LINKS * b)
                dve.wait_ge(x_in, 16 * (b + 1))
                for t in range(TT):
                    st = nc.vector.bn_stats(stats[:, t, :], x_ln[:, t, :])
                link(st)
                nc.vector.memset(rtmp[:], 0.0)
                for t in range(TT):
                    st = nc.vector.bn_aggr(mv[:, t, :], stats[:, t, :])
                link(st)
                deviation(link, mv[:, :, 1], rstd[:], rtmp[:])
                if not isinstance(b, int) or b:
                    dve.wait_ge(xn_tr, b)
                for t in range(TT):
                    st = nc.vector.tensor_scalar(xn[:, t, :], x_ln[:, t, :], mv[:, t, 0:1], rstd[:, t:t + 1],
                                                 ALU.subtract, ALU.mult)
                st.then_inc(xn_done, 1)

            def modulate(b):
                dve.wait_ge(xn_tr, b + 1)
                q = bass.ds((b % 2) * S, S)
                for c in range(DC):
                    args = (tr[:, c, :], mod[:, CA, c, bass.ds(b, 1)], mod[:, SA, c, bass.ds(b, 1)])
                    nc.vector.tensor_scalar(h_next[:, c, :], *args, ALU.mult, ALU.add)
                    if c == 0 and (not isinstance(b, int) or b >= 2):
                        dve.wait_ge(v_made, (b - 1) * NH)
                    m = nc.vector.tensor_scalar(h_hi[:, c, q], *args, ALU.mult, ALU.add)
                m.then_inc(hn_done, 1)
                dve.wait_ge(hn_done, b + 1)
                lo(h_lo[:, :, q], h_next[:], h_hi[:, :, q]).then_inc(h_lo_done, 1)

            normalise(0)
            dve.wait_ge(mod_made, 1)
            mps = bank[1][:, 0:MODS * B].rearrange("p (k c b) -> p k c b", k=6, c=DC)
            link(mod_chain, nc.vector.tensor_copy(mod[:, SA, :, 0:B], mps[:, SA]))
            link(mod_chain, nc.vector.tensor_scalar(mod[:, CA, :, 0:B], mps[:, CA], 1.0, None, ALU.add))
            modulate(0)
            nc.vector.tensor_scalar(ones[:], ident[:], 0.0, 1.0, ALU.mult, ALU.add).then_inc(ones_done, 1)
            dve.wait_ge(mod_made, 2)
            mps2 = bank[5][:, 0:MODS * B].rearrange("p (k c b) -> p k c b", k=6, c=DC)
            link(mod_chain, nc.vector.tensor_copy(mod[:, SB, :, 0:B], mps2[:, SB]))
            link(mod_chain, nc.vector.tensor_scalar(mod[:, CB, :, 0:B], mps2[:, CB], 1.0, None, ALU.add))
            gate(GA, mps2[:, GA])
            gate(GB, mps2[:, GB])
            nc.vector.memset(mtmp[:, 0, 0, 0:1], 0.0).then_inc(mod_ready, 1)

            def step(b, h):
                i = b * NH + h
                first = isinstance(b, int)
                new = not first or i < UNITS

                def has(lag):
                    return not first or 0 <= i - lag < UNITS

                if new:
                    dve.wait_ge(qk_hi_done, i + 1)
                    lo(qk_lo[:, h % 2], qk_ps[h % 2], qk_hi[:, h % 2]).then_inc(qk_lo_done, 1)
                r = (h - 1) % 2
                if has(1):
                    dve.wait_ge(s_made, i)
                    nc.vector.tensor_reduce(smax[:, r, :], s_ps[r], AX_X, ALU.max).then_inc(smax_done, 1)
                    dve.wait_ge(smax_done, i)
                    nc.vector.tensor_scalar(nmax[:, r, :], smax[:, r, :], -SCALE, None,
                                            ALU.mult).then_inc(nmax_done, 1)
                if has(3):
                    r3 = (h - 3) % 2
                    if not first or i >= 5:
                        dve.wait_ge(o_lo_done, i - 4)
                    dve.wait_ge(qsum_done, i - 2)
                    nc.vector.tensor_tensor(vals[:, r3, :], v_ps[r3][:, 0, :], qsum[:, r3, :],
                                            ALU.mult).then_inc(vals_done, 1)
                if (not first or b >= 1) and h == STEP_Y:
                    dve.wait_ge(wo_done, b * NH)
                    if not first or b >= 2:
                        dve.wait_ge(y_tr, b - 1)
                    for c in range(DC):
                        m = nc.vector.tensor_scalar(yT[:, c, :], acc[:, c, :], mod[:, GA, c, bass.ds(b - 1, 1)],
                                                    None, ALU.mult)
                    m.then_inc(y_done, 1)
                if (not first or b >= 1) and h == STEP_X1:
                    dve.wait_ge(y_tr, b)
                    dve.wait_ge(xres_in, 16 * b)
                    nc.vector.tensor_tensor(x1[:, bass.ds(TT * (b - 1), TT), :], x_res[:], tr,
                                            ALU.add).then_inc(x1_done, 1)
                if new and h == STEP_LN:
                    normalise(b + 1)
                if new and h == STEP_HN:
                    modulate(b + 1)
                if has(1):
                    dve.wait_ge(exp_done, i)
                    nc.vector.reciprocal(rinv[:, r, :], rsum[:, r, :]).then_inc(rinv_done, 1)
                    dve.wait_ge(rinv_done, i)
                    nc.vector.tensor_scalar(psum_half[:, r, :], probs[:, r, 0, :], rinv[:, r, 0:1], None,
                                            ALU.mult).then_inc(half_done, 1)
                    if not first or i >= 3:
                        dve.wait_ge(psum_lo_done, i - 2)
                    dve.wait_ge(half_done, i)
                    nc.vector.scalar_tensor_tensor(psum[:, r, :], probs[:, r, 1, :], rinv[:, r, 1:2],
                                                   psum_half[:, r, :], ALU.mult, ALU.add).then_inc(psum_done, 1)
                if has(3):
                    dve.wait_ge(o_hi_done, i - 2)
                    lo(o_lo[:, r3, :], vals[:, r3, :], o_hi[:, r3, :]).then_inc(o_lo_done, 1)

            for h in range(NH):
                step(0, h)
            with dve.Fori(1, B) as b:
                for h in range(NH):
                    step(b, h)
            for h in range(STEP_X1 + 1):
                step(B, h)

            def normalise2(g):
                rows = x1[:, g * TPT:(g + 1) * TPT, :]
                for t in range(TPT):
                    st = nc.vector.bn_stats(stats2[:, t, :], rows[:, t, :])
                link(ln2_chain, st)
                for t in range(TPT):
                    st = nc.vector.bn_aggr(mv2[:, t, :], stats2[:, t, :])
                link(ln2_chain, st)
                deviation(lambda ins: link(ln2_chain, ins), mv2[:, :, 1], rstd2, rtmp2)
                if g:
                    dve.wait_ge(xn2_tr, g)
                for t in range(TPT):
                    st = nc.vector.tensor_scalar(xn2[:, t, :], rows[:, t, :], mv2[:, t, 0:1],
                                                 rstd2[:, t:t + 1], ALU.subtract, ALU.mult)
                st.then_inc(xn2_done, 1)

            def modulate2(g):
                dve.wait_ge(xn2_tr, g + 1)
                if g:
                    dve.wait_ge(h2_hi_done, g)
                for c in range(DC):
                    for k in range(BPT):
                        b, q = g * BPT + k, slice(k * S, (k + 1) * S)
                        m = nc.vector.tensor_scalar(h2[:, c, q], bank[5 + c][:, q], mod[:, CB, c, b:b + 1],
                                                    mod[:, SB, c, b:b + 1], ALU.mult, ALU.add)
                m.then_inc(h2_done, 1)
                dve.wait_ge(h2_hi_done, g + 1)
                q = slice(g * NT, (g + 1) * NT)
                lo(h2_lo[:, :, q], h2[:], h2_hi[:, :, q]).then_inc(h2_lo_done, 1)

            def wide(ap, n=E):
                return ap.unsqueeze(2).to_broadcast([P, TPT, n])

            def expert_weights(g):
                tt, ts, red = nc.vector.tensor_tensor, nc.vector.tensor_scalar, nc.vector.tensor_reduce
                dve.wait_ge(lg_made, g + 1)
                logit = bank[7][:, 0:TPT * GP].rearrange("p (t e) -> p t e", t=TPT)
                link(gate_chain, red(m1, logit[:, :, 0:E], AX_X, ALU.max))
                link(gate_chain, tt(pe_[:, :, 0:E], logit[:, :, 0:E], wide(m1), ALU.subtract))
                ts(pe_[:, :, E:G], logit[:, :, E:G], -1.0, None, ALU.mult).then_inc(gate_sub, 1)
                dve.wait_ge(gate_exp, g + 1)
                link(gate_chain, red(rr, pe_[:, :, 0:E], AX_X, ALU.add))
                link(gate_chain, nc.vector.reciprocal(rr, rr))
                link(gate_chain, tt(pr, pe_[:, :, 0:E], wide(rr), ALU.mult))

                def largest(src, m, sel):
                    link(gate_chain, red(m, src, AX_X, ALU.max))
                    link(gate_chain, tt(sel, src, wide(m), ALU.is_equal))
                    link(gate_chain, tt(sel, sel, order, ALU.mult))
                    link(gate_chain, red(kk, sel, AX_X, ALU.max))
                    link(gate_chain, tt(sel, sel, wide(kk), ALU.is_equal))

                if g == 0:
                    dve.wait_ge(rank_in, 16)
                largest(pr, m1, sel1)
                link(gate_chain, nc.vector.scalar_tensor_tensor(tmp8, sel1, -2.0, pr, ALU.mult, ALU.add))
                largest(tmp8, m2, sel2)
                link(gate_chain, tt(rr, m1, m2, ALU.add))
                link(gate_chain, nc.vector.reciprocal(rr, rr))
                link(gate_chain, tt(sel1, sel1, sel2, ALU.add))
                link(gate_chain, tt(sel1, sel1, pr, ALU.mult))
                link(gate_chain, tt(comb[:, :, 0:E], sel1, wide(rr), ALU.mult))
                link(gate_chain, ts(m1, pe_[:, :, E], 1.0, None, ALU.add))
                link(gate_chain, nc.vector.reciprocal(comb[:, :, E], m1))
                link(gate_chain, nc.vector.tensor_copy(comb_r, comb))
                if g:
                    dve.wait_ge(comb_tr, g)
                nc.vector.tensor_copy(comb2[:, :, 0:G], f32(comb_r))
                link(gate_chain, tt(comb[:, :, :], comb, f32(comb_r), ALU.subtract))
                nc.vector.tensor_copy(comb2[:, :, G:2 * G], comb).then_inc(comb_done, 1)

            def product_lo(i, j):
                n = rows_of[j]
                dve.wait_ge(f_hi_done, i + 1)
                r = j % 2
                lo(f_lo[0:n, j % 2, :], fu[0:n, r, :], f_hi[0:n, j % 2, :]).then_inc(f_lo_done, 1)

            def product(i, j, first):
                n = rows_of[j]
                r = j % 2
                if not first or i >= 2:
                    dve.wait_ge(f_lo_done, i - 1)
                dve.wait_ge(silu_done, i + 1)
                dve.wait_ge(u_made, i + 1)
                nc.vector.tensor_tensor(fu[0:n, r, :], fs[0:n, :], bank[1][0:n, :], ALU.mult).then_inc(fu_done, 1)
                dve.wait_ge(fu_done, i + 1)
                dve.wait_ge(c_made, i + 1)
                nc.vector.tensor_tensor(fu[0:n, r, :], fu[0:n, r, :], bank[2][0:n, :], ALU.mult).then_inc(fc_done, 1)

            def scaled_output(t):
                dve.wait_ge(d_made, (t + 1) * FT)
                if not (isinstance(t, int) and t == 0):
                    dve.wait_ge(y2_tr, t)
                for c in range(DC):
                    for k in range(BPT):
                        q = slice(k * S, (k + 1) * S)
                        m = nc.vector.tensor_scalar(y2T[:, c, q], bank[3 + c][:, q],
                                                    mod[:, GB, c, bass.ds(BPT * t + k, 1)], None, ALU.mult)
                m.then_inc(y2_done, 1)

            def residual(t):
                dve.wait_ge(y2_tr, t + 1)
                if not (isinstance(t, int) and t == 0):
                    dve.wait_ge(out_done, 16 * t)
                for k in range(2):
                    src = bank[5 + k][:].rearrange("p (c s) -> p c s", c=2)
                    m = nc.vector.tensor_tensor(x2[:, 2 * k:2 * k + 2, :], x1[:, bass.ds(t * TPT + 2 * k, 2), :],
                                                src, ALU.add)
                m.then_inc(x2_done, 1)

            dve.wait_ge(x1_done, B)
            dve.wait_ge(gw_tr, 1)
            gps = bank[7][:, 0:DC * GP].rearrange("p (c g) -> p c g", c=DC)
            link(gate_chain, nc.vector.memset(gwT, 0.0))
            link(gate_chain, nc.vector.tensor_copy(gwT[:, :, 0:G], gps[:, :, 0:G]))
            nc.vector.tensor_copy(gw_hi[:], gwT).then_inc(gw_done, 1)
            dve.wait_ge(gw_done, 1)
            lo(gw_lo[:], gwT, gw_hi[:]).then_inc(gw_done, 1)
            normalise2(0)
            modulate2(0)
            expert_weights(0)
            normalise2(1)
            for j in range(FT):
                if j:
                    product_lo(j - 1, j - 1)
                product(j, j, True)
                g, k = 1 + j // 4, j % 4
                if g < TILES:
                    if k == 0:
                        modulate2(g)
                    if k == 1:
                        expert_weights(g)
                    if k == 3 and g + 1 < TILES:
                        normalise2(g + 1)
            with dve.Fori(1, TILES) as t:
                for j in range(FT):
                    i = t * FT + j
                    product_lo(i - 1, (j - 1) % FT)
                    product(i, j, False)
                    if j == 0:
                        scaled_output(t - 1)
                    if j == 2:
                        residual(t - 1)
            product_lo(TILES * FT - 1, FT - 1)
            scaled_output(TILES - 1)
            residual(TILES - 1)

        @block.gpsimd
        def _(pool):
            def split_head(h):
                pool.wait_ge(w_hi_done, h + 1)
                raw = wraw[:, h % SLOTS, :]
                nc.gpsimd.tensor_tensor(wq_lo[:, h].rearrange("p a c d -> p (a c d)"), raw[:, 0:3 * D],
                                        f32(wq_hi[:, h].rearrange("p a c d -> p (a c d)")), ALU.subtract)
                nc.gpsimd.tensor_tensor(wo_lo[:, h, :], raw[:, 3 * D:4 * D], f32(wo_hi[:, h, :]),
                                        ALU.subtract).then_inc(w_lo_done, 1)

            def psum_lo_part(i, r):
                pool.wait_ge(psum_hi_done, i + 1)
                nc.gpsimd.tensor_tensor(psum_lo[:, r, :], psum[:, r, :], f32(psum_hi[:, r, :]),
                                        ALU.subtract).then_inc(psum_lo_done, 1)

            for h in range(3):
                split_head(h)
            for h in range(NH):
                if h + 3 < NH:
                    split_head(h + 3)
                psum_lo_part(h, h % 2)
            with pool.Fori(1, B) as b:
                for h in range(NH):
                    psum_lo_part(b * NH + h, h % 2)
            for j in range(FT):
                n = rows_of[j]
                f = slice(j * P, j * P + n)
                pool.wait_ge(gu_hi_done, j + 1)
                nc.gpsimd.tensor_tensor(g_lo[:, :, f], graw[:, :, f], f32(g_hi[:, :, f]), ALU.subtract)
                nc.gpsimd.tensor_tensor(u_lo[:, :, f], uraw[:, :, f], f32(u_hi[:, :, f]),
                                        ALU.subtract).then_inc(gu_lo_done, 1)
                pool.wait_ge(d_hi_done, j + 1)
                nc.gpsimd.tensor_tensor(d_lo[0:n, j, :], draw[0:n, j, :], f32(d_hi[0:n, j, :]),
                                        ALU.subtract).then_inc(d_lo_done, 1)


_INS = ["L0_attn_x", "L0_attn_w_qkv", "L0_attn_w_o", "L0_ffn_gate_w", "L0_ffn_w_gate", "L0_ffn_w_up",
        "L0_ffn_w_down", "L0_ffn_shgate_w", "L0_ffn_shw_gate", "L0_ffn_shw_up", "L0_ffn_shw_down",
        "L0_c", "L0_wmod"]


def kernel(**inputs):
    import numpy as np
    import concourse.bacc as bacc
    from concourse.bass_utils import run_bass_kernel_spmd

    arrays = {name: np.ascontiguousarray(inputs[name]) for name in _INS}
    experts, _, hidden = arrays["L0_ffn_w_gate"].shape
    features = experts * hidden + arrays["L0_ffn_shw_gate"].shape[1]
    spread = np.zeros((2, experts + 1, -(-features // P) * P), np.float32)
    for e in range(experts):
        spread[:, e, e * hidden:(e + 1) * hidden] = 1
    spread[:, experts, experts * hidden:features] = 1
    arrays["ident"] = np.eye(P, dtype=np.float32)
    arrays["spread"] = spread.reshape(2 * (experts + 1), -1)
    ranks = np.arange(experts, 0, -1, dtype=np.float32)
    arrays["order"] = np.tile(ranks, (P, 512 // P))

    nc = bacc.Bacc("TRN2", target_bir_lowering=False, num_devices=1)
    args = [nc.dram_tensor(f"in_{n}", a.shape, mybir.dt.from_np(a.dtype), kind="ExternalInput").ap()
            for n, a in arrays.items()]
    out = nc.dram_tensor("out", arrays["L0_attn_x"].shape, F32, kind="ExternalOutput").ap()
    adaln_block(nc, *args, out)
    r = run_bass_kernel_spmd(nc, [{f"in_{n}": a for n, a in arrays.items()}], core_ids=[0])
    return r.results[0]["out"]
```

```python
from contextlib import ExitStack

import concourse.bass as bass
from concourse import mybir

P = 128
ALU = mybir.AluOpType
ACT = mybir.ActivationFunctionType
F32 = mybir.dt.float32
I32 = mybir.dt.int32
F32R = mybir.dt.float32r
AX_X = mybir.AxisListType.X
LN_EPS = 1e-5
NEWTON = 3
LN_LINKS = 5 + 3 * NEWTON
GATE_MIN = 0.25
SA, CA, GA, SB, CB, GB = range(6)


def adaln_block(nc, x, w_qkv, w_o, gate_w, w_gate, w_up, w_down, shgate_w, shw_gate, shw_up,
                shw_down, cond, wmod, ident_in, spread_in, order_in, out):
    B, S, D = x.shape
    HD = w_o.shape[0]
    DH = P
    NH = HD // DH
    DC = D // P
    TT = S // P
    E, _, H = w_gate.shape
    HS = shw_gate.shape[1]
    NF = E * H + HS
    FT = -(-NF // P)
    FE = E * H // P
    NT = 512
    TILES = B * S // NT
    TPT = NT // P
    BPT = NT // S
    SCALE = float(DH) ** -0.5
    G = E + 1
    GP = G + G % 2
    UNITS = B * NH
    SLOTS = 4
    assert DC == 2 and TT == 2 and S == 256 and NH % 2 == 0 and FE * P == E * H
    rows_of = [min(P, NF - j * P) for j in range(FT)]

    ctx = ExitStack()
    with ctx:
        keep, early, late = ctx.enter_context(ExitStack()), ExitStack(), ExitStack()

        def sb(where, name, shape, dt=F32):
            return where.enter_context(nc.sbuf_tensor(name, shape, dt))

        def sem(name):
            return ctx.enter_context(nc.semaphore(name))

        ident = sb(keep, "ident", [P, P])
        mod = sb(keep, "mod", [P, 6, DC, B + 1])
        x1 = sb(keep, "x1", [P, B * TT, D])
        wraw = sb(keep, "wraw", [P, SLOTS, 4 * D])
        wq_hi = sb(early, "wq_hi", [P, NH, 3, DC, DH], F32R)
        wq_lo = sb(early, "wq_lo", [P, NH, 3, DC, DH], F32R)
        wo_hi = sb(early, "wo_hi", [P, NH, D], F32R)
        wo_lo = sb(early, "wo_lo", [P, NH, D], F32R)
        qk_hi = sb(early, "qk_hi", [P, 2, 2, S], F32R)
        qk_lo = sb(early, "qk_lo", [P, 2, 2, S], F32R)
        h_hi = sb(early, "h_hi", [P, DC, 2 * S], F32R)
        h_lo = sb(early, "h_lo", [P, DC, 2 * S], F32R)
        h_next = sb(early, "h_next", [P, DC, S])
        x_ln = sb(early, "x_ln", [P, TT, D])
        xn = sb(early, "xn", [P, TT, D])
        x_res = sb(early, "x_res", [P, TT, D])
        probs = sb(early, "probs", [P, 2, TT, S])
        psum_half = sb(early, "psum_half", [P, 2, S])
        psum = sb(early, "psum", [P, 2, S])
        psum_hi = sb(early, "psum_hi", [P, 2, S], F32R)
        psum_lo = sb(early, "psum_lo", [P, 2, S], F32R)
        ones = sb(early, "ones", [P, P], F32R)
        qsum = sb(early, "qsum", [P, 2, S])
        vals = sb(early, "vals", [P, 2, S])
        o_hi = sb(early, "o_hi", [P, 2, S], F32R)
        o_lo = sb(early, "o_lo", [P, 2, S], F32R)
        yT = sb(early, "yT", [P, DC, S])
        stats = sb(early, "stats", [P, TT, 6])
        mv = sb(early, "mv", [P, TT, 2])
        rstd = sb(early, "rstd", [P, TT])
        rtmp = sb(early, "rtmp", [P, TT])
        smax = sb(early, "smax", [P, 2, TT])
        nmax = sb(early, "nmax", [P, 2, TT])
        rsum = sb(early, "rsum", [P, 2, TT])
        rinv = sb(early, "rinv", [P, 2, TT])
        early.close()
        wmod_sb = x1[:, 0:DC * 6, :].rearrange("p a b -> p (a b)").rearrange("p (c n) -> p c n", c=DC)
        c_sb = x1[0:B, DC * 6, :]
        cTs = x1[:, DC * 6 + 1, 0:DC * B].rearrange("p (c b) -> p c b", c=DC)
        mtmp = x1[:, DC * 6 + 2, 0:2 * DC * B].rearrange("p (a c b) -> p a c b", a=2, c=DC)
        assert DC * 6 + 3 <= B * TT
        raws = ExitStack()
        graw = sb(raws, "graw", [P, DC, NF])
        uraw = sb(raws, "uraw", [P, DC, NF])
        raws.close()
        g_lo = sb(late, "g_lo", [P, DC, NF], F32R)
        u_lo = sb(late, "u_lo", [P, DC, NF], F32R)
        g_hi = sb(late, "g_hi", [P, DC, NF], F32R)
        u_hi = sb(late, "u_hi", [P, DC, NF], F32R)
        d_hi = sb(late, "d_hi", [P, FT, D], F32R)
        d_lo = sb(late, "d_lo", [P, FT, D], F32R)
        h2_hi = sb(late, "h2_hi", [P, DC, B * S], F32R)
        h2_lo = sb(late, "h2_lo", [P, DC, B * S], F32R)
        h2 = sb(late, "h2", [P, DC, NT])
        xn2 = sb(late, "xn2", [P, TPT, D])
        f_hi = sb(late, "f_hi", [P, 2, NT], F32R)
        f_lo = sb(late, "f_lo", [P, 2, NT], F32R)
        fs = sb(late, "fs", [P, NT])
        fu = sb(late, "fu", [P, 2, NT])
        gw_hi = sb(late, "gw_hi", [P, DC, GP], F32R)
        gw_lo = sb(late, "gw_lo", [P, DC, GP], F32R)
        combT = sb(late, "combT", [2 * G, B * S], F32R)
        spread = sb(late, "spread", [2 * G, FT * P], F32R)
        late_small = sb(late, "late_small", [P, 1024])
        sb_combr = sb(late, "comb_r", [P, TPT, G], F32R)
        y2T = h2
        x2 = xn2
        late.close()
        draw = wraw[:].rearrange("p a b -> p (a b)")[:, 0:FT * D].rearrange("p (j d) -> p j d", j=FT)
        spread_raw = fs[0:2 * G, :]
        gw_sb = late_small[0:G, 0:D]
        gwT = late_small[:, D:D + DC * GP].rearrange("p (c g) -> p c g", c=DC)
        off = [D + 32]

        def small(n):
            a = off[0]
            off[0] += n
            return late_small[:, a:a + n]

        order = small(TPT * E).rearrange("p (t e) -> p t e", t=TPT)
        lg = small(TPT * GP).rearrange("p (t e) -> p t e", t=TPT)
        pe_ = small(TPT * GP).rearrange("p (t e) -> p t e", t=TPT)
        pr = small(TPT * E).rearrange("p (t e) -> p t e", t=TPT)
        sel1 = small(TPT * E).rearrange("p (t e) -> p t e", t=TPT)
        sel2 = small(TPT * E).rearrange("p (t e) -> p t e", t=TPT)
        tmp8 = small(TPT * E).rearrange("p (t e) -> p t e", t=TPT)
        comb = small(TPT * G).rearrange("p (t e) -> p t e", t=TPT)
        comb2 = small(TPT * 2 * G).rearrange("p (t e) -> p t e", t=TPT)
        comb_r = sb_combr[:]
        m1, m2, kk, rr = (small(TPT) for _ in range(4))
        stats2 = small(TPT * 6).rearrange("p (t e) -> p t e", t=TPT)
        mv2 = small(TPT * 2).rearrange("p (t e) -> p t e", t=TPT)
        rstd2 = small(TPT)
        rtmp2 = small(TPT)
        assert off[0] <= 1024

        bank = [ctx.enter_context(nc.psum_tensor(f"bank{i}", [P, 512], F32)) for i in range(8)]
        qk_ps = [bank[i][:].rearrange("p (a s) -> p a s", a=2) for i in (0, 1)]
        s_ps = [bank[i][:].rearrange("p (t s) -> p t s", t=TT) for i in (2, 3)]
        v_ps = [bank[i][:].rearrange("p (a s) -> p a s", a=2) for i in (4, 5)]
        acc = bank[6][:].rearrange("p (c s) -> p c s", c=DC)
        tr = bank[7][:].rearrange("p (c s) -> p c s", c=2)

        cst_in = sem("cst_in")
        wmod_in = [sem(f"wmod_in{i}") for i in range(2)]
        c_tr = sem("c_tr")
        c_copied = sem("c_copied")
        c_silu = sem("c_silu")
        mod_made = sem("mod_made")
        mod_chain = sem("mod_chain")
        mod_ready = sem("mod_ready")
        x_in = sem("x_in")
        xres_in = sem("xres_in")
        w_in = [sem(f"w_in{i}") for i in range(SLOTS)]
        w_hi_done = sem("w_hi_done")
        w_lo_done = sem("w_lo_done")
        ln_chain = sem("ln_chain")
        xn_done = sem("xn_done")
        xn_tr = sem("xn_tr")
        hn_done = sem("hn_done")
        h_hi_done = sem("h_hi_done")
        h_lo_done = sem("h_lo_done")
        qk_made = sem("qk_made")
        qk_hi_done = sem("qk_hi_done")
        qk_lo_done = sem("qk_lo_done")
        v_made = sem("v_made")
        s_made = sem("s_made")
        smax_done = sem("smax_done")
        nmax_done = sem("nmax_done")
        exp_done = sem("exp_done")
        rinv_done = sem("rinv_done")
        half_done = sem("half_done")
        psum_done = sem("psum_done")
        psum_hi_done = sem("psum_hi_done")
        psum_lo_done = sem("psum_lo_done")
        ones_done = sem("ones_done")
        qsum_done = sem("qsum_done")
        vals_done = sem("vals_done")
        o_hi_done = sem("o_hi_done")
        o_lo_done = sem("o_lo_done")
        wo_done = sem("wo_done")
        y_done = sem("y_done")
        y_tr = sem("y_tr")
        x1_done = sem("x1_done")
        fw_in = sem("fw_in")
        dw_in = sem("dw_in")
        small_in = sem("small_in")
        rank_in = sem("rank_in")
        piece_in = sem("piece_in")
        spread_done = sem("spread_done")
        gw_tr = sem("gw_tr")
        gw_done = sem("gw_done")
        gu_hi_done = sem("gu_hi_done")
        gu_lo_done = sem("gu_lo_done")
        d_hi_done = sem("d_hi_done")
        d_lo_done = sem("d_lo_done")
        ln2_chain = sem("ln2_chain")
        xn2_done = sem("xn2_done")
        xn2_tr = sem("xn2_tr")
        h2_done = sem("h2_done")
        h2_hi_done = sem("h2_hi_done")
        h2_lo_done = sem("h2_lo_done")
        lg_made = sem("lg_made")
        gate_chain = sem("gate_chain")
        gate_sub = sem("gate_sub")
        gate_exp = sem("gate_exp")
        comb_done = sem("comb_done")
        comb_tr = sem("comb_tr")
        combT_done = sem("combT_done")
        g_made = sem("g_made")
        u_made = sem("u_made")
        c_made = sem("c_made")
        silu_done = sem("silu_done")
        fu_done = sem("fu_done")
        fc_done = sem("fc_done")
        f_hi_done = sem("f_hi_done")
        f_lo_done = sem("f_lo_done")
        d_made = sem("d_made")
        y2_done = sem("y2_done")
        y2_tr = sem("y2_tr")
        x2_done = sem("x2_done")
        out_done = sem("out_done")

        def f32(ap):
            return ap.bitcast(F32)

        x_v = x.rearrange("b (t p) d -> b p t d", p=P)
        out_v = out.rearrange("b (t p) d -> p (b t) d", p=P)
        wqkv_v = w_qkv.rearrange("(c p) (a h d) -> h p a c d", p=P, a=3, h=NH)
        wo_v = w_o.rearrange("(h p) n -> h p n", p=P)
        MODS = 6 * DC

        LAG = dict(scores=1, smax=1, exp=2, qsum_p=3, v=4, qsum=5, vals=5, split=6, wo=7)
        STEP_Y = LAG["wo"]
        STEP_LN, STEP_YT, STEP_X1, STEP_XT, STEP_HN = STEP_Y + 1, STEP_Y + 2, STEP_Y + 3, STEP_Y + 4, STEP_Y + 5

        def turn(b, h, lag, stage):
            bb, g = (b, h - lag) if h >= lag else (b - 1, h - lag + NH)
            if not isinstance(b, int) or (0 <= bb < B):
                stage(bb, g, bb * NH + g)

        def wait(eng, s, value):
            if not isinstance(value, int) or value > 0:
                eng.wait_ge(s, value)

        block = ctx.enter_context(nc.Block())

        @block.sync
        def _(sp):
            sp.dma_start(ident[:], ident_in).then_inc(cst_in, 16)
            sp.dma_start(c_sb, cond).then_inc(cst_in, 16)
            wmod_v = wmod.rearrange("(c p) n -> p c n", p=P)
            sp.dma_start(wmod_sb[:, :, 0:2 * D], wmod_v[:, :, 0:2 * D]).then_inc(wmod_in[0], 16)
            sp.dma_start(x_ln[:], x_v[0]).then_inc(x_in, 16)

            def head_weights(h):
                if h >= SLOTS:
                    sp.wait_ge(w_lo_done, h - SLOTS + 1)
                slot = wraw[:, h % SLOTS, :]
                dst = slot[:, 0:3 * D].rearrange("p (a c d) -> p a c d", a=3, c=DC)
                for a in range(3):
                    sp.dma_start(dst[:, a], wqkv_v[h][:, a]).then_inc(w_in[h % SLOTS], 16)
                sp.dma_start(slot[:, 3 * D:4 * D], wo_v[h]).then_inc(w_in[h % SLOTS], 16)

            head_weights(0)
            head_weights(1)
            sp.dma_start(wmod_sb[:, :, 2 * D:6 * D], wmod_v[:, :, 2 * D:6 * D]).then_inc(wmod_in[1], 16)
            sp.dma_start(x_res[:], x_v[0]).then_inc(xres_in, 16)
            for h in range(2, NH):
                head_weights(h)
                if h == SLOTS:
                    sp.wait_ge(xn_done, 1)
                    sp.dma_start(x_ln[:], x_v[1]).then_inc(x_in, 16)
            sp.wait_ge(w_lo_done, NH)
            sp.dma_start(draw[:, 0:FE, :], w_down.rearrange("e h d -> (e h) d").rearrange(
                "(j p) d -> p j d", p=P)).then_inc(dw_in, 16)
            full = HS // P
            sp.dma_start(draw[:, FE:FE + full, :], shw_down[0:full * P, :].rearrange(
                "(j p) d -> p j d", p=P)).then_inc(dw_in, 16)
            sp.dma_start(draw[0:HS - full * P, FE + full, :], shw_down[full * P:HS, :]).then_inc(dw_in, 16)
            with sp.Fori(1, B - 1) as b:
                sp.wait_ge(xn_done, b + 1)
                sp.dma_start(x_ln[:], x_v[b + 1]).then_inc(x_in, 16)
                sp.wait_ge(x1_done, b)
                sp.dma_start(x_res[:], x_v[b]).then_inc(xres_in, 16)
            sp.wait_ge(xn_done, B)
            sp.dma_start(x_ln[:], x_v[B - 1]).then_inc(x_in, 16)
            sp.wait_ge(x1_done, B - 1)
            sp.dma_start(x_res[:], x_v[B - 1]).then_inc(xres_in, 16)

            sp.wait_ge(qk_made, UNITS)
            sp.wait_ge(v_made, UNITS)
            for raw, w, shw in ((graw, w_gate, shw_gate), (uraw, w_up, shw_up)):
                for c in range(DC):
                    sp.dma_start(raw[:, c, 0:E * H].rearrange("p (e h) -> p e h", e=E),
                                 w[:, c * P:(c + 1) * P, :].rearrange("e p h -> p e h")).then_inc(fw_in, 16)
                sp.dma_start(raw[:, :, E * H:NF], shw.rearrange("(c p) h -> p c h", p=P)).then_inc(fw_in, 16)
            sp.wait_ge(x1_done, B)
            sp.dma_start(gw_sb[0:E, :], gate_w).then_inc(small_in, 16)
            sp.dma_start(gw_sb[E:G, :], shgate_w.rearrange("(a d) -> a d", a=1)).then_inc(small_in, 16)
            sp.dma_start(order, order_in.rearrange("p (t e) -> p t e", t=TPT)).then_inc(rank_in, 16)
            for q in range(0, FT * P, NT):
                n = min(NT, FT * P - q)
                if q:
                    sp.wait_ge(spread_done, q // NT)
                sp.dma_start(spread_raw[:, 0:n], spread_in[:, q:q + n]).then_inc(piece_in, 16)
            with sp.Fori(0, TILES) as t:
                sp.wait_ge(x2_done, t + 1)
                sp.dma_start(out_v[:, bass.ds(t * TPT, TPT), :], x2[:]).then_inc(out_done, 16)
            sp.wait_ge(out_done, 16 * TILES)

        @block.tensor
        def _(pe):
            def three(dst, lhs, rhs, start, stop, skip=False):
                n = len(lhs)
                for k in range(n):
                    for m, (i, j) in enumerate(((0, 0), (1, 0), (0, 1))):
                        mm = nc.tensor.matmul(dst, lhs[k][i], rhs[k][j], start=start and k == 0 and m == 0,
                                              stop=stop and k == n - 1 and m == 2, skip_group_check=skip)
                return mm

            pe.wait_ge(cst_in, 32)
            for c in range(DC):
                mm = nc.tensor.transpose(bank[0][:, c * B:(c + 1) * B], c_sb[:, c * P:(c + 1) * P], ident[0:B, 0:B])
            mm.then_inc(c_tr, 1)
            pe.wait_ge(c_silu, 1)

            def modulations(part, ps, chunks):
                pe.wait_ge(wmod_in[part], 16)
                for m in chunks:
                    for c in range(DC):
                        mm = nc.tensor.matmul(ps[:, m * B:(m + 1) * B], wmod_sb[:, c, m * P:(m + 1) * P],
                                              cTs[:, c, :], start=c == 0, stop=c == DC - 1)
                mm.then_inc(mod_made, 1)

            modulations(0, bank[1], range(2 * DC))

            def x_transposes(b):
                pe.wait_ge(xn_done, b + 1)
                if not isinstance(b, int) or b >= 2:
                    pe.wait_ge(x1_done, b - 1)
                elif b == 1:
                    pe.wait_ge(mod_ready, 1)
                for c in range(DC):
                    for t in range(TT):
                        mm = nc.tensor.transpose(tr[:, c, t * P:(t + 1) * P], xn[:, t, c * P:(c + 1) * P], ident[:])
                mm.then_inc(xn_tr, 1)

            def y_transposes(b):
                pe.wait_ge(y_done, b + 1)
                pe.wait_ge(hn_done, min(b + 2, B) if isinstance(b, int) else b + 2)
                for t in range(TT):
                    for c in range(DC):
                        mm = nc.tensor.transpose(tr[:, t, c * P:(c + 1) * P], yT[:, c, t * P:(t + 1) * P], ident[:])
                mm.then_inc(y_tr, 1)

            def queries_keys(b, g, u):
                if isinstance(b, int) and b == 0:
                    pe.wait_ge(w_lo_done, g + 1)
                if g == 0:
                    pe.wait_ge(h_lo_done, b + 1)
                wait(pe, qk_lo_done, u - 1)
                for a in range(2):
                    mm = three(qk_ps[g % 2][:, a, :],
                               [(wq_hi[:, g, a, c, :], wq_lo[:, g, a, c, :]) for c in range(DC)],
                               act_rows(b), True, True)
                mm.then_inc(qk_made, 1)

            def act_rows(b):
                q = bass.ds((b % 2) * S, S)
                return [(h_hi[:, c, q], h_lo[:, c, q]) for c in range(DC)]

            def scores(b, g, u):
                r = g % 2
                pe.wait_ge(qk_lo_done, u + 1)
                wait(pe, exp_done, u - 1)
                for t in range(TT):
                    q = slice(t * P, (t + 1) * P)
                    mm = three(s_ps[r][:, t, :], [(qk_hi[:, r, 0, q], qk_lo[:, r, 0, q])],
                               [(qk_hi[:, r, 1, :], qk_lo[:, r, 1, :])], True, True)
                mm.then_inc(s_made, 1)

            def values(b, g, u):
                r = g % 2
                if isinstance(b, int) and u == 0:
                    pe.wait_ge(ones_done, 1)
                wait(pe, vals_done, u - 1)
                three(v_ps[r][:, 0, :], [(wq_hi[:, g, 2, c, :], wq_lo[:, g, 2, c, :]) for c in range(DC)],
                      act_rows(b), True, True)
                pe.wait_ge(psum_lo_done, u + 1)
                nc.tensor.matmul(v_ps[r][:, 1, :], ones[:], psum_hi[:, r, :], start=True, stop=False)
                nc.tensor.matmul(v_ps[r][:, 1, :], ones[:], psum_lo[:, r, :], start=False,
                                 stop=True).then_inc(v_made, 1)

            def project(b, g, u):
                if g == 0:
                    wait(pe, y_done, b)
                pe.wait_ge(o_lo_done, u + 1)
                for c in range(DC):
                    f = slice(c * P, (c + 1) * P)
                    mm = three(acc[:, c, :], [(wo_hi[:, g, f], wo_lo[:, g, f])],
                               [(o_hi[:, g % 2, :], o_lo[:, g % 2, :])], g == 0 and c == 0,
                               g == NH - 1 and c == DC - 1, skip=True)
                mm.then_inc(wo_done, 1)

            def step(b, h):
                turn(b, h, 0, queries_keys)
                turn(b, h, LAG["scores"], scores)
                turn(b, h, LAG["wo"], project)
                turn(b, h, LAG["v"], values)
                if h == STEP_XT and not (isinstance(b, int) and b == B):
                    x_transposes(b + 1)
                if h == STEP_YT and not (isinstance(b, int) and b == 0):
                    y_transposes(b - 1)

            x_transposes(0)
            for h in range(NH):
                step(0, h)
                if h == 1:
                    pe.wait_ge(hn_done, 1)
                    modulations(1, bank[7], range(2 * DC, MODS))
            with pe.Fori(1, B) as b:
                for h in range(NH):
                    step(b, h)
            for h in range(STEP_YT + 1):
                step(B, h)

            tra, trb = (bank[i][:].rearrange("p (c s) -> p c s", c=2) for i in (5, 6))
            acc2 = [bank[3], bank[4]]

            pe.wait_ge(small_in, 32)
            pe.wait_ge(x1_done, B)
            for c in range(DC):
                mm = nc.tensor.transpose(bank[7][:, c * GP:c * GP + G], gw_sb[:, c * P:(c + 1) * P], ident[0:G, 0:G])
            mm.then_inc(gw_tr, 1)

            def rows_transposes(g):
                pe.wait_ge(xn2_done, g + 1)
                if g:
                    pe.wait_ge(h2_done, g)
                for c in range(DC):
                    for t in range(TPT):
                        mm = nc.tensor.transpose((bank[5], bank[6])[c][:, t * P:(t + 1) * P],
                                                 xn2[:, t, c * P:(c + 1) * P], ident[:])
                mm.then_inc(xn2_tr, 1)

            def logits(g):
                pe.wait_ge(h2_lo_done, g + 1)
                if g == 0:
                    pe.wait_ge(gw_done, 2)
                else:
                    pe.wait_ge(combT_done, g)
                for t in range(TPT):
                    q = slice((g * TPT + t) * P, (g * TPT + t + 1) * P)
                    mm = three(bank[7][:, t * GP:(t + 1) * GP],
                               [(h2_hi[:, c, q], h2_lo[:, c, q]) for c in range(DC)],
                               [(gw_hi[:, c, :], gw_lo[:, c, :]) for c in range(DC)], True, True)
                mm.then_inc(lg_made, 1)

            def comb_transposes(g):
                pe.wait_ge(comb_done, g + 1)
                for t in range(TPT):
                    mm = nc.tensor.transpose(bank[7][0:2 * G, t * P:(t + 1) * P], comb2[:, t, :], ident[:])
                mm.then_inc(comb_tr, 1)

            def features(t, j, first):
                i = t * FT + j
                n = rows_of[j]
                f = slice(j * P, j * P + n)
                rhs = [(h2_hi[:, c, bass.ds(t * NT, NT)], h2_lo[:, c, bass.ds(t * NT, NT)]) for c in range(DC)]
                if first:
                    pe.wait_ge(gu_lo_done, j + 1)
                if first and j == 0:
                    pe.wait_ge(h2_lo_done, 1)
                if not first or i:
                    pe.wait_ge(silu_done, i)
                three(bank[0][0:n, :], [(g_hi[:, c, f], g_lo[:, c, f]) for c in range(DC)], rhs,
                      True, True).then_inc(g_made, 1)
                if not first or i:
                    pe.wait_ge(fu_done, i)
                    pe.wait_ge(fc_done, i)
                if first and j == 0:
                    pe.wait_ge(combT_done, 1)
                    pe.wait_ge(spread_done, -(-FT * P // NT))
                three(bank[1][0:n, :], [(u_hi[:, c, f], u_lo[:, c, f]) for c in range(DC)], rhs,
                      True, True).then_inc(u_made, 1)
                nc.tensor.matmul(bank[2][0:n, :], spread[:, f], combT[:, bass.ds(t * NT, NT)],
                                 start=True, stop=True).then_inc(c_made, 1)

            def down(t, j, first, i):
                n = rows_of[j]
                if first or j == FT - 1:
                    pe.wait_ge(d_lo_done, j + 1)
                pe.wait_ge(f_lo_done, i + 1)
                if j == 0 and not (isinstance(t, int) and t == 0):
                    pe.wait_ge(y2_done, t)
                for c in range(DC):
                    q = slice(c * P, (c + 1) * P)
                    mm = three(acc2[c][:], [(d_hi[0:n, j, q], d_lo[0:n, j, q])],
                               [(f_hi[0:n, j % 2, :], f_lo[0:n, j % 2, :])], j == 0, j == FT - 1, skip=True)
                mm.then_inc(d_made, 1)

            def out_transposes(t):
                pe.wait_ge(y2_done, t + 1)
                if not (isinstance(t, int) and t == 0):
                    pe.wait_ge(x2_done, t)
                for k in range(TPT):
                    for c in range(DC):
                        mm = nc.tensor.transpose((tra, trb)[k // 2][:, k % 2, c * P:(c + 1) * P],
                                                 y2T[:, c, k * P:(k + 1) * P], ident[:])
                mm.then_inc(y2_tr, 1)

            rows_transposes(0)
            logits(0)
            comb_transposes(0)
            for j in range(FT):
                features(0, j, True)
                if j:
                    down(0, j - 1, True, j - 1)
                g, k = 1 + j // 4, j % 4
                if g < TILES:
                    if k == 0:
                        rows_transposes(g)
                    if k == 1:
                        logits(g)
                    if k == 3:
                        comb_transposes(g)
            with pe.Fori(1, TILES) as t:
                for j in range(FT):
                    features(t, j, False)
                    if j == 0:
                        down(t - 1, FT - 1, False, t * FT - 1)
                    else:
                        down(t, j - 1, False, t * FT + j - 1)
                    if j == 2:
                        out_transposes(t - 1)
            down(TILES - 1, FT - 1, False, TILES * FT - 1)
            out_transposes(TILES - 1)


        @block.scalar
        def _(act):
            act.wait_ge(c_tr, 1)
            nc.scalar.activation(cTs, bank[0][:, 0:DC * B].rearrange("p (c b) -> p c b", c=DC),
                                 ACT.Silu).then_inc(c_silu, 1)

            def copy(dst, src):
                return nc.scalar.activation(dst, src, ACT.Copy)

            def split_head(h):
                act.wait_ge(w_in[h % SLOTS], 64 * (h // SLOTS + 1))
                raw = wraw[:, h % SLOTS, :]
                copy(wq_hi[:, h].rearrange("p a c d -> p (a c d)"), raw[:, 0:3 * D])
                copy(wo_hi[:, h, :], raw[:, 3 * D:4 * D]).then_inc(w_hi_done, 1)

            def split_qk(b, g, u):
                act.wait_ge(qk_made, u + 1)
                wait(act, s_made, u - 1)
                copy(qk_hi[:, g % 2], qk_ps[g % 2]).then_inc(qk_hi_done, 1)

            def exponentials(b, g, u):
                r = g % 2
                wait(act, psum_done, u - 1)
                act.wait_ge(nmax_done, u + 1)
                for t in range(TT):
                    e = nc.scalar.activation(probs[:, r, t, :], s_ps[r][:, t, :], ACT.Exp,
                                             bias=nmax[:, r, t:t + 1], scale=SCALE,
                                             accum_out=rsum[:, r, t:t + 1])
                e.then_inc(exp_done, 1)

            def split_psum(b, g, u):
                wait(act, v_made, u - 1)
                act.wait_ge(psum_done, u + 1)
                copy(psum_hi[:, g % 2, :], psum[:, g % 2, :]).then_inc(psum_hi_done, 1)

            def query_sums(b, g, u):
                wait(act, vals_done, u - 1)
                act.wait_ge(v_made, u + 1)
                copy(qsum[:, g % 2, :], v_ps[g % 2][:, 1, :]).then_inc(qsum_done, 1)

            def split_values(b, g, u):
                wait(act, wo_done, u - 1)
                act.wait_ge(vals_done, u + 1)
                copy(o_hi[:, g % 2, :], vals[:, g % 2, :]).then_inc(o_hi_done, 1)

            def step(b, h):
                turn(b, h, LAG["qsum"], query_sums)
                turn(b, h, LAG["split"], split_values)
                turn(b, h, LAG["exp"], exponentials)
                turn(b, h, 0, split_qk)
                turn(b, h, LAG["qsum_p"], split_psum)
                if isinstance(b, int) and b == 0 and h + 3 < NH:
                    split_head(h + 3)

            split_head(0)
            split_head(1)
            split_head(2)
            for h in range(NH):
                step(0, h)
            with act.Fori(1, B) as b:
                for h in range(NH):
                    step(b, h)
            for h in range(LAG["wo"]):
                step(B, h)

            def split_down(j):
                n = rows_of[j]
                if j == 0:
                    act.wait_ge(dw_in, 48)
                copy(d_hi[0:n, j, :], draw[0:n, j, :]).then_inc(d_hi_done, 1)

            def split_features(j):
                f = slice(j * P, j * P + rows_of[j])
                if j == 0:
                    act.wait_ge(fw_in, 96)
                copy(g_hi[:, :, f], graw[:, :, f])
                copy(u_hi[:, :, f], uraw[:, :, f]).then_inc(gu_hi_done, 1)

            def rows2_hi(g):
                act.wait_ge(h2_done, g + 1)
                copy(h2_hi[:, :, g * NT:(g + 1) * NT], h2[:]).then_inc(h2_hi_done, 1)

            def gates_exp(g):
                act.wait_ge(gate_sub, g + 1)
                nc.scalar.activation(pe_[:, :, 0:G], pe_[:, :, 0:G], ACT.Exp).then_inc(gate_exp, 1)

            def comb_out(g):
                act.wait_ge(comb_tr, g + 1)
                copy(combT[:, g * NT:(g + 1) * NT], bank[7][0:2 * G, 0:NT]).then_inc(combT_done, 1)

            def product_hi(i, j, first):
                n = rows_of[j]
                act.wait_ge(fc_done, i + 1)
                if not first or i >= 2:
                    act.wait_ge(d_made, i - 1)
                r = j % 2
                copy(f_hi[0:n, j % 2, :], fu[0:n, r, :]).then_inc(f_hi_done, 1)

            def silu(i, j, first):
                n = rows_of[j]
                act.wait_ge(g_made, i + 1)
                if not first or i:
                    act.wait_ge(fu_done, i)
                nc.scalar.activation(fs[0:n, :], bank[0][0:n, :], ACT.Silu).then_inc(silu_done, 1)

            act.wait_ge(x1_done, B)
            pieces = -(-FT * P // NT)
            for k in range(pieces):
                act.wait_ge(piece_in, 16 * (k + 1))
                q, n = k * NT, min(NT, FT * P - k * NT)
                copy(spread[:, q:q + n], spread_raw[:, 0:n]).then_inc(spread_done, 1)
            split_features(0)
            split_down(0)
            rows2_hi(0)
            split_features(1)
            split_down(1)
            gates_exp(0)
            comb_out(0)
            for j in range(FT):
                if j:
                    product_hi(j - 1, j - 1, True)
                silu(j, j, True)
                if j + 2 < FT:
                    split_features(j + 2)
                    split_down(j + 2)
                g, k = 1 + j // 4, j % 4
                if g < TILES:
                    if k == 0:
                        rows2_hi(g)
                    if k == 1:
                        gates_exp(g)
                    if k == 3:
                        comb_out(g)
            with act.Fori(1, TILES) as t:
                for j in range(FT):
                    i = t * FT + j
                    product_hi(i - 1, (j - 1) % FT, False)
                    silu(i, j, False)
            product_hi(TILES * FT - 1, FT - 1, False)

        @block.vector
        def _(dve):
            def lo(dst, src, hi):
                return nc.vector.tensor_tensor(dst, src, f32(hi), ALU.subtract)

            chains = {}

            def link(s, ins):
                chains[s.name] = chains.get(s.name, 0) + 1
                ins.then_inc(s, 1)
                dve.wait_ge(s, chains[s.name])

            def counted(s, base):
                n = [0]

                def link(ins):
                    n[0] += 1
                    ins.then_inc(s, 1)
                    dve.wait_ge(s, base + n[0])

                return link

            def deviation(link, v, y, t):
                ts, stt = nc.vector.tensor_scalar, nc.vector.scalar_tensor_tensor
                link(ts(v, v, LN_EPS, None, ALU.add))
                link(ts(t.bitcast(I32), v.bitcast(I32), 1, None, ALU.arith_shift_right))
                link(ts(y.bitcast(I32), t.bitcast(I32), -1.0, float(0x5F3759DF), ALU.mult, ALU.add))
                for _ in range(NEWTON):
                    link(stt(t, y, -0.5, y, ALU.mult, ALU.mult))
                    link(nc.vector.tensor_tensor(t, t, v, ALU.mult))
                    link(stt(y, t, 1.5, y, ALU.add, ALU.mult))

            link(mod_chain, nc.vector.memset(mod[:], 0.0))

            def gate(k, src):
                sgn, mag = mtmp[:, 0], mtmp[:, 1]
                link(mod_chain, nc.vector.tensor_scalar(sgn, src, 0.0, 2.0, ALU.is_ge, ALU.mult))
                link(mod_chain, nc.vector.tensor_scalar(sgn, sgn, -1.0, None, ALU.add))
                link(mod_chain, nc.vector.tensor_tensor(mag, sgn, src, ALU.mult))
                link(mod_chain, nc.vector.tensor_scalar(mag, mag, GATE_MIN, None, ALU.max))
                link(mod_chain, nc.vector.tensor_tensor(mod[:, k, :, 0:B], sgn, mag, ALU.mult))

            def normalise(b):
                link = counted(ln_chain, LN_LINKS * b)
                dve.wait_ge(x_in, 16 * (b + 1))
                for t in range(TT):
                    st = nc.vector.bn_stats(stats[:, t, :], x_ln[:, t, :])
                link(st)
                nc.vector.memset(rtmp[:], 0.0)
                for t in range(TT):
                    st = nc.vector.bn_aggr(mv[:, t, :], stats[:, t, :])
                link(st)
                deviation(link, mv[:, :, 1], rstd[:], rtmp[:])
                if not isinstance(b, int) or b:
                    dve.wait_ge(xn_tr, b)
                for t in range(TT):
                    st = nc.vector.tensor_scalar(xn[:, t, :], x_ln[:, t, :], mv[:, t, 0:1], rstd[:, t:t + 1],
                                                 ALU.subtract, ALU.mult)
                st.then_inc(xn_done, 1)

            def modulate(b):
                dve.wait_ge(xn_tr, b + 1)
                q = bass.ds((b % 2) * S, S)
                for c in range(DC):
                    args = (tr[:, c, :], mod[:, CA, c, bass.ds(b, 1)], mod[:, SA, c, bass.ds(b, 1)])
                    nc.vector.tensor_scalar(h_next[:, c, :], *args, ALU.mult, ALU.add)
                    if c == 0 and (not isinstance(b, int) or b >= 2):
                        dve.wait_ge(v_made, (b - 1) * NH)
                    m = nc.vector.tensor_scalar(h_hi[:, c, q], *args, ALU.mult, ALU.add)
                m.then_inc(hn_done, 1)
                dve.wait_ge(hn_done, b + 1)
                lo(h_lo[:, :, q], h_next[:], h_hi[:, :, q]).then_inc(h_lo_done, 1)

            normalise(0)
            dve.wait_ge(mod_made, 1)
            mps = bank[1][:, 0:MODS * B].rearrange("p (k c b) -> p k c b", k=6, c=DC)
            link(mod_chain, nc.vector.tensor_copy(mod[:, SA, :, 0:B], mps[:, SA]))
            link(mod_chain, nc.vector.tensor_scalar(mod[:, CA, :, 0:B], mps[:, CA], 1.0, None, ALU.add))
            modulate(0)
            nc.vector.tensor_scalar(ones[:], ident[:], 0.0, 1.0, ALU.mult, ALU.add).then_inc(ones_done, 1)
            def split_qk(b, g, u):
                dve.wait_ge(qk_hi_done, u + 1)
                lo(qk_lo[:, g % 2], qk_ps[g % 2], qk_hi[:, g % 2]).then_inc(qk_lo_done, 1)

            def row_max(b, g, u):
                r = g % 2
                dve.wait_ge(s_made, u + 1)
                nc.vector.tensor_reduce(smax[:, r, :], s_ps[r], AX_X, ALU.max).then_inc(smax_done, 1)
                dve.wait_ge(smax_done, u + 1)
                nc.vector.tensor_scalar(nmax[:, r, :], smax[:, r, :], -SCALE, None, ALU.mult).then_inc(nmax_done, 1)

            def row_inverse(b, g, u):
                dve.wait_ge(exp_done, u + 1)
                nc.vector.reciprocal(rinv[:, g % 2, :], rsum[:, g % 2, :]).then_inc(rinv_done, 1)

            def half_sum(b, g, u):
                r = g % 2
                dve.wait_ge(rinv_done, u + 1)
                nc.vector.tensor_scalar(psum_half[:, r, :], probs[:, r, 0, :], rinv[:, r, 0:1], None,
                                        ALU.mult).then_inc(half_done, 1)

            def full_sum(b, g, u):
                r = g % 2
                wait(dve, psum_lo_done, u - 1)
                dve.wait_ge(half_done, u + 1)
                nc.vector.scalar_tensor_tensor(psum[:, r, :], probs[:, r, 1, :], rinv[:, r, 1:2],
                                               psum_half[:, r, :], ALU.mult, ALU.add).then_inc(psum_done, 1)

            def times_v(b, g, u):
                r = g % 2
                wait(dve, o_lo_done, u - 1)
                dve.wait_ge(qsum_done, u + 1)
                nc.vector.tensor_tensor(vals[:, r, :], v_ps[r][:, 0, :], qsum[:, r, :],
                                        ALU.mult).then_inc(vals_done, 1)

            def gated_output(b):
                dve.wait_ge(wo_done, (b + 1) * NH)
                wait(dve, y_tr, b)
                for c in range(DC):
                    m = nc.vector.tensor_scalar(yT[:, c, :], acc[:, c, :], mod[:, GA, c, bass.ds(b, 1)],
                                                None, ALU.mult)
                m.then_inc(y_done, 1)

            def residual1(b):
                dve.wait_ge(y_tr, b + 1)
                dve.wait_ge(xres_in, 16 * (b + 1))
                nc.vector.tensor_tensor(x1[:, bass.ds(TT * b, TT), :], x_res[:], tr, ALU.add).then_inc(x1_done, 1)

            def other_modulations():
                dve.wait_ge(mod_made, 2)
                mps2 = bank[7][:, 0:MODS * B].rearrange("p (k c b) -> p k c b", k=6, c=DC)
                link(mod_chain, nc.vector.tensor_copy(mod[:, SB, :, 0:B], mps2[:, SB]))
                link(mod_chain, nc.vector.tensor_scalar(mod[:, CB, :, 0:B], mps2[:, CB], 1.0, None, ALU.add))
                gate(GA, mps2[:, GA])
                gate(GB, mps2[:, GB])
                nc.vector.memset(mtmp[:, 0, 0, 0:1], 0.0).then_inc(mod_ready, 1)

            def step(b, h):
                last = isinstance(b, int) and b == B
                some = not (isinstance(b, int) and b == 0)
                if some and h == STEP_Y:
                    gated_output(b - 1)
                turn(b, h, LAG["qsum_p"], row_inverse)
                turn(b, h, LAG["vals"], times_v)
                turn(b, h, LAG["qsum_p"], half_sum)
                turn(b, h, LAG["qsum_p"], full_sum)
                turn(b, h, LAG["smax"], row_max)
                turn(b, h, 0, split_qk)
                if not some and h == 2:
                    other_modulations()
                if some and h == STEP_X1:
                    residual1(b - 1)
                if not last and h == STEP_LN:
                    normalise(b + 1)
                if not last and h == STEP_HN:
                    modulate(b + 1)

            for h in range(NH):
                step(0, h)
            with dve.Fori(1, B) as b:
                for h in range(NH):
                    step(b, h)
            for h in range(STEP_X1 + 1):
                step(B, h)

            def normalise2(g):
                rows = x1[:, g * TPT:(g + 1) * TPT, :]
                for t in range(TPT):
                    st = nc.vector.bn_stats(stats2[:, t, :], rows[:, t, :])
                link(ln2_chain, st)
                for t in range(TPT):
                    st = nc.vector.bn_aggr(mv2[:, t, :], stats2[:, t, :])
                link(ln2_chain, st)
                deviation(lambda ins: link(ln2_chain, ins), mv2[:, :, 1], rstd2, rtmp2)
                if g:
                    dve.wait_ge(xn2_tr, g)
                for t in range(TPT):
                    st = nc.vector.tensor_scalar(xn2[:, t, :], rows[:, t, :], mv2[:, t, 0:1],
                                                 rstd2[:, t:t + 1], ALU.subtract, ALU.mult)
                st.then_inc(xn2_done, 1)

            def modulate2(g):
                dve.wait_ge(xn2_tr, g + 1)
                if g:
                    dve.wait_ge(h2_hi_done, g)
                for c in range(DC):
                    for k in range(BPT):
                        b, q = g * BPT + k, slice(k * S, (k + 1) * S)
                        m = nc.vector.tensor_scalar(h2[:, c, q], bank[5 + c][:, q], mod[:, CB, c, b:b + 1],
                                                    mod[:, SB, c, b:b + 1], ALU.mult, ALU.add)
                m.then_inc(h2_done, 1)
                dve.wait_ge(h2_hi_done, g + 1)
                q = slice(g * NT, (g + 1) * NT)
                lo(h2_lo[:, :, q], h2[:], h2_hi[:, :, q]).then_inc(h2_lo_done, 1)

            def wide(ap, n=E):
                return ap.unsqueeze(2).to_broadcast([P, TPT, n])

            def expert_weights(g):
                tt, ts, red = nc.vector.tensor_tensor, nc.vector.tensor_scalar, nc.vector.tensor_reduce
                dve.wait_ge(lg_made, g + 1)
                logit = bank[7][:, 0:TPT * GP].rearrange("p (t e) -> p t e", t=TPT)
                link(gate_chain, red(m1, logit[:, :, 0:E], AX_X, ALU.max))
                link(gate_chain, tt(pe_[:, :, 0:E], logit[:, :, 0:E], wide(m1), ALU.subtract))
                ts(pe_[:, :, E:G], logit[:, :, E:G], -1.0, None, ALU.mult).then_inc(gate_sub, 1)
                dve.wait_ge(gate_exp, g + 1)
                link(gate_chain, red(rr, pe_[:, :, 0:E], AX_X, ALU.add))
                link(gate_chain, nc.vector.reciprocal(rr, rr))
                link(gate_chain, tt(pr, pe_[:, :, 0:E], wide(rr), ALU.mult))

                def largest(src, m, sel):
                    link(gate_chain, red(m, src, AX_X, ALU.max))
                    link(gate_chain, tt(sel, src, wide(m), ALU.is_equal))
                    link(gate_chain, tt(sel, sel, order, ALU.mult))
                    link(gate_chain, red(kk, sel, AX_X, ALU.max))
                    link(gate_chain, tt(sel, sel, wide(kk), ALU.is_equal))

                if g == 0:
                    dve.wait_ge(rank_in, 16)
                largest(pr, m1, sel1)
                link(gate_chain, nc.vector.scalar_tensor_tensor(tmp8, sel1, -2.0, pr, ALU.mult, ALU.add))
                largest(tmp8, m2, sel2)
                link(gate_chain, tt(rr, m1, m2, ALU.add))
                link(gate_chain, nc.vector.reciprocal(rr, rr))
                link(gate_chain, tt(sel1, sel1, sel2, ALU.add))
                link(gate_chain, tt(sel1, sel1, pr, ALU.mult))
                link(gate_chain, tt(comb[:, :, 0:E], sel1, wide(rr), ALU.mult))
                link(gate_chain, ts(m1, pe_[:, :, E], 1.0, None, ALU.add))
                link(gate_chain, nc.vector.reciprocal(comb[:, :, E], m1))
                link(gate_chain, nc.vector.tensor_copy(comb_r, comb))
                if g:
                    dve.wait_ge(comb_tr, g)
                nc.vector.tensor_copy(comb2[:, :, 0:G], f32(comb_r))
                link(gate_chain, tt(comb[:, :, :], comb, f32(comb_r), ALU.subtract))
                nc.vector.tensor_copy(comb2[:, :, G:2 * G], comb).then_inc(comb_done, 1)

            def product_lo(i, j):
                n = rows_of[j]
                dve.wait_ge(f_hi_done, i + 1)
                r = j % 2
                lo(f_lo[0:n, j % 2, :], fu[0:n, r, :], f_hi[0:n, j % 2, :]).then_inc(f_lo_done, 1)

            def product(i, j, first):
                n = rows_of[j]
                r = j % 2
                if not first or i >= 2:
                    dve.wait_ge(f_lo_done, i - 1)
                dve.wait_ge(silu_done, i + 1)
                dve.wait_ge(u_made, i + 1)
                nc.vector.tensor_tensor(fu[0:n, r, :], fs[0:n, :], bank[1][0:n, :], ALU.mult).then_inc(fu_done, 1)
                dve.wait_ge(fu_done, i + 1)
                dve.wait_ge(c_made, i + 1)
                nc.vector.tensor_tensor(fu[0:n, r, :], fu[0:n, r, :], bank[2][0:n, :], ALU.mult).then_inc(fc_done, 1)

            def scaled_output(t):
                dve.wait_ge(d_made, (t + 1) * FT)
                if not (isinstance(t, int) and t == 0):
                    dve.wait_ge(y2_tr, t)
                for c in range(DC):
                    for k in range(BPT):
                        q = slice(k * S, (k + 1) * S)
                        m = nc.vector.tensor_scalar(y2T[:, c, q], bank[3 + c][:, q],
                                                    mod[:, GB, c, bass.ds(BPT * t + k, 1)], None, ALU.mult)
                m.then_inc(y2_done, 1)

            def residual(t):
                dve.wait_ge(y2_tr, t + 1)
                if not (isinstance(t, int) and t == 0):
                    dve.wait_ge(out_done, 16 * t)
                for k in range(2):
                    src = bank[5 + k][:].rearrange("p (c s) -> p c s", c=2)
                    m = nc.vector.tensor_tensor(x2[:, 2 * k:2 * k + 2, :], x1[:, bass.ds(t * TPT + 2 * k, 2), :],
                                                src, ALU.add)
                m.then_inc(x2_done, 1)

            dve.wait_ge(x1_done, B)
            dve.wait_ge(gw_tr, 1)
            gps = bank[7][:, 0:DC * GP].rearrange("p (c g) -> p c g", c=DC)
            link(gate_chain, nc.vector.memset(gwT, 0.0))
            link(gate_chain, nc.vector.tensor_copy(gwT[:, :, 0:G], gps[:, :, 0:G]))
            nc.vector.tensor_copy(gw_hi[:], gwT).then_inc(gw_done, 1)
            dve.wait_ge(gw_done, 1)
            lo(gw_lo[:], gwT, gw_hi[:]).then_inc(gw_done, 1)
            normalise2(0)
            modulate2(0)
            expert_weights(0)
            normalise2(1)
            for j in range(FT):
                if j:
                    product_lo(j - 1, j - 1)
                product(j, j, True)
                g, k = 1 + j // 4, j % 4
                if g < TILES:
                    if k == 0:
                        modulate2(g)
                    if k == 1:
                        expert_weights(g)
                    if k == 3 and g + 1 < TILES:
                        normalise2(g + 1)
            with dve.Fori(1, TILES) as t:
                for j in range(FT):
                    i = t * FT + j
                    product_lo(i - 1, (j - 1) % FT)
                    product(i, j, False)
                    if j == 0:
                        scaled_output(t - 1)
                    if j == 2:
                        residual(t - 1)
            product_lo(TILES * FT - 1, FT - 1)
            scaled_output(TILES - 1)
            residual(TILES - 1)

        @block.gpsimd
        def _(pool):
            def split_head(h):
                pool.wait_ge(w_hi_done, h + 1)
                raw = wraw[:, h % SLOTS, :]
                nc.gpsimd.tensor_tensor(wq_lo[:, h].rearrange("p a c d -> p (a c d)"), raw[:, 0:3 * D],
                                        f32(wq_hi[:, h].rearrange("p a c d -> p (a c d)")), ALU.subtract)
                nc.gpsimd.tensor_tensor(wo_lo[:, h, :], raw[:, 3 * D:4 * D], f32(wo_hi[:, h, :]),
                                        ALU.subtract).then_inc(w_lo_done, 1)

            def split_psum(b, g, u):
                r = g % 2
                pool.wait_ge(psum_hi_done, u + 1)
                nc.gpsimd.tensor_tensor(psum_lo[:, r, :], psum[:, r, :], f32(psum_hi[:, r, :]),
                                        ALU.subtract).then_inc(psum_lo_done, 1)

            def split_values(b, g, u):
                r = g % 2
                pool.wait_ge(o_hi_done, u + 1)
                nc.gpsimd.tensor_tensor(o_lo[:, r, :], vals[:, r, :], f32(o_hi[:, r, :]),
                                        ALU.subtract).then_inc(o_lo_done, 1)

            def step(b, h):
                turn(b, h, LAG["split"], split_values)
                turn(b, h, LAG["qsum_p"], split_psum)

            for h in range(3):
                split_head(h)
            for h in range(NH):
                step(0, h)
                if h + 3 < NH:
                    split_head(h + 3)
            with pool.Fori(1, B) as b:
                for h in range(NH):
                    step(b, h)
            for h in range(LAG["split"]):
                step(B, h)
            for j in range(FT):
                n = rows_of[j]
                f = slice(j * P, j * P + n)
                pool.wait_ge(gu_hi_done, j + 1)
                nc.gpsimd.tensor_tensor(g_lo[:, :, f], graw[:, :, f], f32(g_hi[:, :, f]), ALU.subtract)
                nc.gpsimd.tensor_tensor(u_lo[:, :, f], uraw[:, :, f], f32(u_hi[:, :, f]),
                                        ALU.subtract).then_inc(gu_lo_done, 1)
                pool.wait_ge(d_hi_done, j + 1)
                nc.gpsimd.tensor_tensor(d_lo[0:n, j, :], draw[0:n, j, :], f32(d_hi[0:n, j, :]),
                                        ALU.subtract).then_inc(d_lo_done, 1)


_INS = ["L0_attn_x", "L0_attn_w_qkv", "L0_attn_w_o", "L0_ffn_gate_w", "L0_ffn_w_gate", "L0_ffn_w_up",
        "L0_ffn_w_down", "L0_ffn_shgate_w", "L0_ffn_shw_gate", "L0_ffn_shw_up", "L0_ffn_shw_down",
        "L0_c", "L0_wmod"]


def kernel(**inputs):
    import numpy as np
    import concourse.bacc as bacc
    from concourse.bass_utils import run_bass_kernel_spmd

    arrays = {name: np.ascontiguousarray(inputs[name]) for name in _INS}
    experts, _, hidden = arrays["L0_ffn_w_gate"].shape
    features = experts * hidden + arrays["L0_ffn_shw_gate"].shape[1]
    spread = np.zeros((2, experts + 1, -(-features // P) * P), np.float32)
    for e in range(experts):
        spread[:, e, e * hidden:(e + 1) * hidden] = 1
    spread[:, experts, experts * hidden:features] = 1
    arrays["ident"] = np.eye(P, dtype=np.float32)
    arrays["spread"] = spread.reshape(2 * (experts + 1), -1)
    ranks = np.arange(experts, 0, -1, dtype=np.float32)
    arrays["order"] = np.tile(ranks, (P, 512 // P))

    nc = bacc.Bacc("TRN2", target_bir_lowering=False, num_devices=1)
    args = [nc.dram_tensor(f"in_{n}", a.shape, mybir.dt.from_np(a.dtype), kind="ExternalInput").ap()
            for n, a in arrays.items()]
    out = nc.dram_tensor("out", arrays["L0_attn_x"].shape, F32, kind="ExternalOutput").ap()
    adaln_block(nc, *args, out)
    r = run_bass_kernel_spmd(nc, [{f"in_{n}": a for n, a in arrays.items()}], core_ids=[0])
    return r.results[0]["out"]
```

```python
from contextlib import ExitStack

import concourse.bass as bass
from concourse import mybir

P = 128
ALU = mybir.AluOpType
ACT = mybir.ActivationFunctionType
F32 = mybir.dt.float32
I32 = mybir.dt.int32
F32R = mybir.dt.float32r
AX_X = mybir.AxisListType.X
LN_EPS = 1e-5
NEWTON = 3
LN_LINKS = 5 + 3 * NEWTON
GATE_MIN = 0.25
SA, CA, GA, SB, CB, GB = range(6)


def adaln_block(nc, x, w_qkv, w_o, gate_w, w_gate, w_up, w_down, shgate_w, shw_gate, shw_up,
                shw_down, cond, wmod, ident_in, spread_in, order_in, out):
    B, S, D = x.shape
    HD = w_o.shape[0]
    DH = P
    NH = HD // DH
    DC = D // P
    TT = S // P
    E, _, H = w_gate.shape
    HS = shw_gate.shape[1]
    NF = E * H + HS
    FT = -(-NF // P)
    FE = E * H // P
    NT = 512
    TILES = B * S // NT
    TPT = NT // P
    BPT = NT // S
    SCALE = float(DH) ** -0.5
    G = E + 1
    GP = G + G % 2
    UNITS = B * NH
    SLOTS = 4
    assert DC == 2 and TT == 2 and S == 256 and NH % 2 == 0 and FE * P == E * H
    rows_of = [min(P, NF - j * P) for j in range(FT)]

    ctx = ExitStack()
    with ctx:
        keep, early, late = ctx.enter_context(ExitStack()), ExitStack(), ExitStack()

        top = {}

        def sb(where, name, shape, dt=F32):
            n = 4
            for s in shape[1:]:
                n *= s
            start[name] = top.get(id(where), 0)
            top[id(where)] = start[name] + n
            return where.enter_context(nc.sbuf_tensor(name, shape, dt))

        start = {}

        def skip_to(where, name):
            n = start[name] - top.get(id(where), 0)
            assert n >= 0, name
            if n:
                sb(where, f"gap{len(start)}_before_{name}", [P, n // 4])

        def sem(name):
            return ctx.enter_context(nc.semaphore(name))

        ident = sb(keep, "ident", [P, P])
        mod = sb(keep, "mod", [P, 6, DC, B])
        x1 = sb(keep, "x1", [P, B * TT, D])
        staging = ExitStack()
        wraw = sb(staging, "wraw", [P, SLOTS, 4 * D])
        staging.close()
        xn2 = sb(keep, "xn2", [P, TPT, D])
        h2 = sb(keep, "h2", [P, DC, NT])
        h2_hi0 = sb(keep, "h2_hi0", [P, DC, NT], F32R)
        h2_lo0 = sb(keep, "h2_lo0", [P, DC, NT], F32R)
        assert SLOTS * 4 * D == (TPT * D) + 3 * DC * NT
        wq_hi = sb(early, "wq_hi", [P, NH, 3, DC, DH], F32R)
        wq_lo = sb(early, "wq_lo", [P, NH, 3, DC, DH], F32R)
        wo_hi = sb(early, "wo_hi", [P, NH, D], F32R)
        wo_lo = sb(early, "wo_lo", [P, NH, D], F32R)
        qk_hi = sb(early, "qk_hi", [P, 2, 2, S], F32R)
        qk_lo = sb(early, "qk_lo", [P, 2, 2, S], F32R)
        h_hi = sb(early, "h_hi", [P, DC, 2 * S], F32R)
        h_lo = sb(early, "h_lo", [P, DC, 2 * S], F32R)
        h_next = sb(early, "h_next", [P, DC, S])
        x_ln = sb(early, "x_ln", [P, TT, D])
        xn = sb(early, "xn", [P, TT, D])
        probs = sb(early, "probs", [P, 2, TT, S])
        psum_half = sb(early, "psum_half", [P, 2, S])
        psum = sb(early, "psum", [P, 2, S])
        psum_hi = sb(early, "psum_hi", [P, 2, S], F32R)
        psum_lo = sb(early, "psum_lo", [P, 2, S], F32R)
        x_res = sb(early, "x_res", [P, TT, D])
        ones = sb(early, "ones", [P, P], F32R)
        qsum = sb(early, "qsum", [P, 2, S])
        vals = sb(early, "vals", [P, 2, S])
        o_hi = sb(early, "o_hi", [P, 2, S], F32R)
        o_lo = sb(early, "o_lo", [P, 2, S], F32R)
        yT = sb(early, "yT", [P, DC, S])
        stats = sb(early, "stats", [P, TT, 6])
        mv = sb(early, "mv", [P, TT, 2])
        rstd = sb(early, "rstd", [P, TT])
        rtmp = sb(early, "rtmp", [P, TT])
        smax = sb(early, "smax", [P, 2, TT])
        nmax = sb(early, "nmax", [P, 2, TT])
        rsum = sb(early, "rsum", [P, 2, TT])
        rinv = sb(early, "rinv", [P, 2, TT])
        early.close()
        wmod_sb = x1[:, 0:DC * 6, :].rearrange("p a b -> p (a b)").rearrange("p (c n) -> p c n", c=DC)
        c_sb = x1[0:B, DC * 6, :]
        cTs = x1[:, DC * 6 + 1, 0:DC * B].rearrange("p (c b) -> p c b", c=DC)
        mtmp = x1[:, DC * 6 + 2, 0:2 * DC * B].rearrange("p (a c b) -> p a c b", a=2, c=DC)
        assert DC * 6 + 3 <= B * TT
        raws = ExitStack()
        graw = sb(raws, "graw", [P, DC, NF])
        uraw = sb(raws, "uraw", [P, DC, NF])
        draw = sb(raws, "draw", [P, FT, D])
        skip_to(raws, "qk_hi")
        spread_raw = sb(raws, "spread_raw", [2 * G, FT * P])
        skip_to(raws, "h_hi")
        logitsT = sb(raws, "logitsT", [GP, B * S])
        raws.close()
        HEAD_BYTES = 3 * D * 4
        graw_heads, uraw_heads = (-(-start[n] // HEAD_BYTES) for n in ("uraw", "draw"))
        draw_heads = -(-(start["draw"] + FT * D * 4) // HEAD_BYTES)
        g_lo = sb(late, "g_lo", [P, DC, NF], F32R)
        u_lo = sb(late, "u_lo", [P, DC, NF], F32R)
        d_lo = sb(late, "d_lo", [P, FT, D], F32R)
        fs = sb(late, "fs", [P, NT])
        fu = sb(late, "fu", [P, 2, NT])
        skip_to(late, "wq_lo")
        g_hi = sb(late, "g_hi", [P, DC, NF], F32R)
        u_hi = sb(late, "u_hi", [P, DC, NF], F32R)
        d_hi = sb(late, "d_hi", [P, FT, D], F32R)
        rest_small = sb(late, "rest_small", [P, (start["wo_hi"] - top[id(late)]) // 4])
        h2_hi = sb(late, "h2_hi", [P, DC, B * S - NT], F32R)
        h2_lo = sb(late, "h2_lo", [P, DC, B * S - NT], F32R)
        skip_to(late, "qk_hi")
        spread = sb(late, "spread", [2 * G, FT * P], F32R)
        skip_to(late, "h_hi")
        combT = sb(late, "combT", [2 * G, B * S], F32R)
        skip_to(late, "h_next")
        late_small = sb(late, "late_small", [P, 688])
        small_r = sb(late, "small_r", [P, 2 * DC * GP + B * TT * G], F32R)
        with nc.sbuf_tensor("logitsT0", [GP, NT], F32) as logitsT0:
            pass
        combT0 = sb(late, "combT0", [2 * G, NT], F32R)
        skip_to(late, "probs")
        f_hi = sb(late, "f_hi", [P, 2, NT], F32R)
        f_lo = sb(late, "f_lo", [P, 2, NT], F32R)
        assert top[id(late)] <= start["psum_hi"]
        gw_hi, gw_lo = (small_r[:, k * DC * GP:(k + 1) * DC * GP].rearrange("p (c g) -> p c g", c=DC)
                        for k in range(2))
        all_r = small_r[:, 2 * DC * GP:].rearrange("p (t e) -> p t e", t=B * TT)
        comb_r = [all_r[:, 0:TPT, :], all_r[:, TPT:, :]]
        y2T = h2
        x2 = xn2
        late.close()
        gw_sb = late_small[0:G, 0:D]
        gwT = late_small[:, D:D + DC * GP].rearrange("p (c g) -> p c g", c=DC)
        order = late_small[:, D + DC * GP:D + DC * GP + E].unsqueeze(1)
        ln2_small = [ap[:, 0:TPT * 10].rearrange("p (t e) -> p t e", t=TPT)
                     for ap in (yT[:, 0, :], rest_small[:, rest_small.shape[1] - TPT * 10:])]

        class Experts:

            def __init__(self, place, first, n, comb_r):
                off = [first]

                def small(*sizes):
                    a = off[0]
                    m = n
                    for s in sizes:
                        m *= s
                    off[0] += m
                    assert off[0] <= place.shape[1]
                    ap = place[:, a:a + m]
                    return ap.rearrange("p (t e) -> p t e", t=n) if sizes else ap

                self.n = n
                self.exps, self.probs, self.masked = small(G), small(E), small(E)
                self.sel1, self.sel2 = small(E), small(E)
                self.comb, self.comb2 = small(G), small(2 * G)
                self.m1, self.m2, self.rank, self.total = (small() for _ in range(4))
                self.comb_r = comb_r

        experts = [Experts(late_small, D + DC * GP + E, TPT, comb_r[0]),
                   Experts(rest_small, 0, B * TT - TPT, comb_r[1])]

        bank = [ctx.enter_context(nc.psum_tensor(f"bank{i}", [P, 512], F32)) for i in range(8)]
        qk_ps = [bank[i][:].rearrange("p (a s) -> p a s", a=2) for i in (0, 1)]
        s_ps = [bank[i][:].rearrange("p (t s) -> p t s", t=TT) for i in (2, 3)]
        v_ps = [bank[i][:].rearrange("p (a s) -> p a s", a=2) for i in (4, 5)]
        acc = bank[6][:].rearrange("p (c s) -> p c s", c=DC)
        tr = bank[7][:].rearrange("p (c s) -> p c s", c=2)

        cst_in = sem("cst_in")
        wmod_in = [sem(f"wmod_in{i}") for i in range(2)]
        c_tr = sem("c_tr")
        c_silu = sem("c_silu")
        mod_made = sem("mod_made")
        mod_chain = sem("mod_chain")
        mod_ready = sem("mod_ready")
        x_in = sem("x_in")
        xres_in = sem("xres_in")
        w_in = [sem(f"w_in{i}") for i in range(SLOTS)]
        w_hi_done = sem("w_hi_done")
        w_lo_done = sem("w_lo_done")
        wo_lo_done = sem("wo_lo_done")
        ln_chain = sem("ln_chain")
        xn_done = sem("xn_done")
        xn_tr = sem("xn_tr")
        hn_done = sem("hn_done")
        h_hi_done = sem("h_hi_done")
        h_lo_done = sem("h_lo_done")
        qk_made = sem("qk_made")
        qk_hi_done = sem("qk_hi_done")
        qk_lo_done = sem("qk_lo_done")
        v_made = sem("v_made")
        s_made = sem("s_made")
        smax_done = sem("smax_done")
        nmax_done = sem("nmax_done")
        exp_done = sem("exp_done")
        rinv_done = sem("rinv_done")
        half_done = sem("half_done")
        psum_done = sem("psum_done")
        psum_hi_done = sem("psum_hi_done")
        psum_lo_done = sem("psum_lo_done")
        ones_done = sem("ones_done")
        qsum_done = sem("qsum_done")
        vals_done = sem("vals_done")
        o_hi_done = sem("o_hi_done")
        o_lo_done = sem("o_lo_done")
        wo_done = sem("wo_done")
        y_done = sem("y_done")
        y_tr = sem("y_tr")
        x1_done = sem("x1_done")
        fw_in = sem("fw_in")
        dw_in = sem("dw_in")
        small_in = sem("small_in")
        rank_in = sem("rank_in")
        spread_in_done = sem("spread_in_done")
        spread_done = sem("spread_done")
        gw_tr = sem("gw_tr")
        gw_done = sem("gw_done")
        gu_hi_done = sem("gu_hi_done")
        gu_lo_done = sem("gu_lo_done")
        d_hi_done = sem("d_hi_done")
        d_lo_done = sem("d_lo_done")
        ln2_chain = sem("ln2_chain")
        xn2_done = sem("xn2_done")
        xn2_tr = sem("xn2_tr")
        h2_done = sem("h2_done")
        half_tr = sem("half_tr")
        half_h2 = sem("half_h2")
        half_hi = sem("half_hi")
        h2_hi_done = sem("h2_hi_done")
        h2_lo_done = sem("h2_lo_done")
        lgT_made = sem("lgT_made")
        lgT_done = sem("lgT_done")
        lg_made = sem("lg_made")
        gate_chain = sem("gate_chain")
        gate_sub = sem("gate_sub")
        gate_exp = sem("gate_exp")
        comb_done = sem("comb_done")
        comb_tr = sem("comb_tr")
        combT_done = sem("combT_done")
        g_made = sem("g_made")
        u_made = sem("u_made")
        c_made = sem("c_made")
        silu_done = sem("silu_done")
        fu_done = sem("fu_done")
        fc_done = sem("fc_done")
        f_hi_done = sem("f_hi_done")
        f_lo_done = sem("f_lo_done")
        d_made = sem("d_made")
        y2_done = sem("y2_done")
        y2_tr = sem("y2_tr")
        x2_done = sem("x2_done")
        out_done = sem("out_done")

        def f32(ap):
            return ap.bitcast(F32)

        x_v = x.rearrange("b (t p) d -> b p t d", p=P)
        out_v = out.rearrange("b (t p) d -> p (b t) d", p=P)
        wqkv_v = w_qkv.rearrange("(c p) (a h d) -> h p a c d", p=P, a=3, h=NH)
        wo_v = w_o.rearrange("(h p) n -> h p n", p=P)
        MODS = 6 * DC

        LAG = dict(scores=1, smax=1, exp=2, qsum_p=3, v=4, qsum=5, vals=5, split=6, wo=7)
        STEP_Y = LAG["wo"]
        STEP_YT, STEP_X1, STEP_XT, STEP_HN = STEP_Y + 2, STEP_Y + 3, STEP_Y + 4, STEP_Y + 5
        MOD_STEP = 5
        STEP_LN = 8

        def turn(b, h, lag, stage):
            bb, g = (b, h - lag) if h >= lag else (b - 1, h - lag + NH)
            if not isinstance(b, int) or (0 <= bb < B):
                stage(bb, g, bb * NH + g)

        def wait(eng, s, value):
            if not isinstance(value, int) or value > 0:
                eng.wait_ge(s, value)

        LN2_STEP, GATE_STEP, ROWS_STEPS = 0, 1, (3, 5)
        LOGITS_STEP, LOGITS_TR_STEP = 8, 11
        CHOICE_STEPS = {(B - 1, 12): (0,), (B - 1, 13): (1,), (B - 1, 14): (2,), (B - 1, 15): (3,),
                        (B, 0): (4, 5)}
        assert ROWS_STEPS[1] + 2 < LOGITS_STEP < STEP_YT and STEP_X1 < LOGITS_TR_STEP
        COMB_STEP, SPREAD_STEP, FFN_STEP = 1, 2, 3
        LAST_YT, LAST_X1 = STEP_Y, STEP_Y + 1
        ROWS_AT = {3: 1, 5: 2, 7: 3}
        NORM_AT = {j: [(g, n) for n in range(a, z)] for j, g, a, z in (
            (0, 1, 0, 2), (1, 1, 2, 10), (2, 1, 10, LN_LINKS + 1), (3, 2, 0, 9), (4, 2, 9, LN_LINKS + 1),
            (5, 3, 0, 9), (6, 3, 9, LN_LINKS + 1))}
        CHOICE_AT = 10
        assert FFN_STEP + min(ROWS_AT) + 3 >= LAST_X1
        assert len(ROWS_AT) == TILES - 1 and max(ROWS_AT) + 3 <= CHOICE_AT

        def at(j, stage, after=0):
            if j - after in ROWS_AT:
                stage(ROWS_AT[j - after])

        def rows_parts(t):
            if isinstance(t, int) and t == 0:
                return h2_hi0, h2_lo0
            q = bass.ds(t * NT - NT, NT)
            return h2_hi[:, :, q], h2_lo[:, :, q]

        comb_banks = ((7,), (7, 5, 6))

        rows_banks = ((7, 7), (5, 7), (5, 6), (5, 6))

        block = ctx.enter_context(nc.Block())

        @block.sync
        def _(sp):
            sp.dma_start(ident[:], ident_in).then_inc(cst_in, 16)
            sp.dma_start(c_sb, cond).then_inc(cst_in, 16)
            wmod_v = wmod.rearrange("(c p) n -> p c n", p=P)
            sp.dma_start(x_ln[:], x_v[0]).then_inc(x_in, 16)
            sp.dma_start(wmod_sb[:, :, 0:2 * D], wmod_v[:, :, 0:2 * D]).then_inc(wmod_in[0], 16)

            def head_weights(h):
                if h >= SLOTS:
                    sp.wait_ge(w_lo_done, h - SLOTS + 1)
                    sp.wait_ge(wo_lo_done, h - SLOTS + 1)
                slot = wraw[:, h % SLOTS, :]
                dst = slot[:, 0:3 * D].rearrange("p (a c d) -> p a c d", a=3, c=DC)
                for a in range(3):
                    sp.dma_start(dst[:, a], wqkv_v[h][:, a]).then_inc(w_in[h % SLOTS], 16)
                sp.dma_start(slot[:, 3 * D:4 * D], wo_v[h]).then_inc(w_in[h % SLOTS], 16)

            head_weights(0)
            for h in range(1, SLOTS - 1):
                head_weights(h)
            sp.dma_start(wmod_sb[:, :, 2 * D:6 * D], wmod_v[:, :, 2 * D:6 * D]).then_inc(wmod_in[1], 16)
            sp.dma_start(x_res[:], x_v[0]).then_inc(xres_in, 16)
            for h in range(SLOTS - 1, NH):
                head_weights(h)
                if h == SLOTS:
                    sp.wait_ge(xn_done, 1)
                    sp.dma_start(x_ln[:], x_v[1]).then_inc(x_in, 16)
            with sp.Fori(1, B - 1) as b:
                sp.wait_ge(xn_done, b + 1)
                sp.dma_start(x_ln[:], x_v[b + 1]).then_inc(x_in, 16)
                sp.wait_ge(x1_done, b)
                sp.dma_start(x_res[:], x_v[b]).then_inc(xres_in, 16)
            sp.wait_ge(h_lo_done, B)
            sp.dma_start(gw_sb[0:E, :], gate_w).then_inc(small_in, 16)
            sp.dma_start(gw_sb[E:G, :], shgate_w.rearrange("(a d) -> a d", a=1)).then_inc(small_in, 16)
            sp.dma_start(order[:, 0, :], order_in).then_inc(rank_in, 16)
            sp.wait_ge(x1_done, B - 1)
            sp.dma_start(x_res[:], x_v[B - 1]).then_inc(xres_in, 16)

            def feature_weights(raw, w, shw):
                for c in range(DC):
                    sp.dma_start(raw[:, c, 0:E * H].rearrange("p (e h) -> p e h", e=E),
                                 w[:, c * P:(c + 1) * P, :].rearrange("e p h -> p e h")).then_inc(fw_in, 16)
                sp.dma_start(raw[:, :, E * H:NF], shw.rearrange("(c p) h -> p c h", p=P)).then_inc(fw_in, 16)

            sp.wait_ge(v_made, UNITS - NH + graw_heads)
            feature_weights(graw, w_gate, shw_gate)
            sp.wait_ge(v_made, UNITS - NH + uraw_heads)
            feature_weights(uraw, w_up, shw_up)
            sp.wait_ge(s_made, UNITS)
            sp.dma_start(spread_raw[:], spread_in).then_inc(spread_in_done, 16)
            sp.wait_ge(v_made, UNITS - NH + draw_heads)
            sp.dma_start(draw[:, 0:FE, :], w_down.rearrange("e h d -> (e h) d").rearrange(
                "(j p) d -> p j d", p=P)).then_inc(dw_in, 16)
            full = HS // P
            sp.dma_start(draw[:, FE:FE + full, :], shw_down[0:full * P, :].rearrange(
                "(j p) d -> p j d", p=P)).then_inc(dw_in, 16)
            sp.dma_start(draw[0:HS - full * P, FE + full, :], shw_down[full * P:HS, :]).then_inc(dw_in, 16)
            with sp.Fori(0, TILES) as t:
                sp.wait_ge(x2_done, t + 1)
                sp.dma_start(out_v[:, bass.ds(t * TPT, TPT), :], x2[:]).then_inc(out_done, 16)
            sp.wait_ge(out_done, 16 * TILES)

        @block.tensor
        def _(pe):
            def three(dst, lhs, rhs, start, stop, skip=False):
                n = len(lhs)
                for k in range(n):
                    for m, (i, j) in enumerate(((0, 0), (1, 0), (0, 1))):
                        mm = nc.tensor.matmul(dst, lhs[k][i], rhs[k][j], start=start and k == 0 and m == 0,
                                              stop=stop and k == n - 1 and m == 2, skip_group_check=skip)
                return mm

            pe.wait_ge(cst_in, 32)
            for c in range(DC):
                mm = nc.tensor.transpose(bank[0][:, c * B:(c + 1) * B], c_sb[:, c * P:(c + 1) * P], ident[0:B, 0:B])
            mm.then_inc(c_tr, 1)
            pe.wait_ge(c_silu, 1)

            def modulations(part, ps, chunks):
                pe.wait_ge(wmod_in[part], 16)
                if part:
                    pe.wait_ge(hn_done, 1)
                for m in chunks:
                    for c in range(DC):
                        mm = nc.tensor.matmul(ps[:, m * B:(m + 1) * B], wmod_sb[:, c, m * P:(m + 1) * P],
                                              cTs[:, c, :], start=c == 0, stop=c == DC - 1)
                mm.then_inc(mod_made, 1)

            modulations(0, bank[1], range(2 * DC))

            def x_transposes(b):
                pe.wait_ge(xn_done, b + 1)
                if not isinstance(b, int) or b >= 2:
                    pe.wait_ge(x1_done, b - 1)
                elif b == 1:
                    pe.wait_ge(mod_ready, 1)
                for c in range(DC):
                    for t in range(TT):
                        mm = nc.tensor.transpose(tr[:, c, t * P:(t + 1) * P], xn[:, t, c * P:(c + 1) * P], ident[:])
                mm.then_inc(xn_tr, 1)

            def y_transposes(b):
                pe.wait_ge(y_done, b + 1)
                if not isinstance(b, int) or b < B - 2:
                    pe.wait_ge(hn_done, b + 2)
                elif b == B - 2:
                    pe.wait_ge(lgT_done, 1)
                else:
                    pe.wait_ge(h2_done, 2)
                for t in range(TT):
                    for c in range(DC):
                        mm = nc.tensor.transpose(tr[:, t, c * P:(c + 1) * P], yT[:, c, t * P:(t + 1) * P], ident[:])
                mm.then_inc(y_tr, 1)

            def queries_keys(b, g, u):
                if isinstance(b, int) and b == 0:
                    pe.wait_ge(w_lo_done, g + 1)
                if g == 0:
                    pe.wait_ge(h_lo_done, b + 1)
                wait(pe, qk_lo_done, u - 1)
                for a in range(2):
                    mm = three(qk_ps[g % 2][:, a, :],
                               [(wq_hi[:, g, a, c, :], wq_lo[:, g, a, c, :]) for c in range(DC)],
                               act_rows(b), True, True)
                mm.then_inc(qk_made, 1)

            def act_rows(b):
                q = bass.ds((b % 2) * S, S)
                return [(h_hi[:, c, q], h_lo[:, c, q]) for c in range(DC)]

            def scores(b, g, u):
                r = g % 2
                pe.wait_ge(qk_lo_done, u + 1)
                wait(pe, exp_done, u - 1)
                for t in range(TT):
                    q = slice(t * P, (t + 1) * P)
                    mm = three(s_ps[r][:, t, :], [(qk_hi[:, r, 0, q], qk_lo[:, r, 0, q])],
                               [(qk_hi[:, r, 1, :], qk_lo[:, r, 1, :])], True, True)
                mm.then_inc(s_made, 1)

            def values(b, g, u):
                r = g % 2
                if isinstance(b, int) and u == 0:
                    pe.wait_ge(ones_done, 1)
                wait(pe, vals_done, u - 1)
                three(v_ps[r][:, 0, :], [(wq_hi[:, g, 2, c, :], wq_lo[:, g, 2, c, :]) for c in range(DC)],
                      act_rows(b), True, True)
                pe.wait_ge(psum_lo_done, u + 1)
                nc.tensor.matmul(v_ps[r][:, 1, :], ones[:], psum_hi[:, r, :], start=True, stop=False)
                nc.tensor.matmul(v_ps[r][:, 1, :], ones[:], psum_lo[:, r, :], start=False,
                                 stop=True).then_inc(v_made, 1)

            def project(b, g, u):
                if isinstance(b, int) and b == 0:
                    pe.wait_ge(wo_lo_done, g + 1)
                if g == 0:
                    wait(pe, y_done, b)
                pe.wait_ge(o_lo_done, u + 1)
                for c in range(DC):
                    f = slice(c * P, (c + 1) * P)
                    mm = three(acc[:, c, :], [(wo_hi[:, g, f], wo_lo[:, g, f])],
                               [(o_hi[:, g % 2, :], o_lo[:, g % 2, :])], g == 0 and c == 0,
                               g == NH - 1 and c == DC - 1, skip=True)
                mm.then_inc(wo_done, 1)

            def step(b, h):
                turn(b, h, 0, queries_keys)
                if isinstance(b, int) and b == 0 and 1 <= h < MOD_STEP:
                    a, n = 2 * DC, (MODS - 2 * DC) // (MOD_STEP - 1)
                    modulations(1, bank[7], range(a + (h - 1) * n, a + h * n))
                turn(b, h, LAG["scores"], scores)
                turn(b, h, LAG["wo"], project)
                turn(b, h, LAG["v"], values)
                if h == STEP_XT and not (isinstance(b, int) and b >= B - 1):
                    x_transposes(b + 1)
                if h == STEP_YT and not (isinstance(b, int) and b == 0):
                    y_transposes(b - 1)

            x_transposes(0)
            for h in range(NH):
                step(0, h)
            with pe.Fori(1, B - 1) as b:
                for h in range(NH):
                    step(b, h)
            tra, trb = (bank[i][:].rearrange("p (c s) -> p c s", c=2) for i in (5, 6))
            acc2 = [bank[3], bank[4]]

            def gate_weights():
                pe.wait_ge(small_in, 32)
                pe.wait_ge(hn_done, B)
                for c in range(DC):
                    mm = nc.tensor.transpose(bank[7][:, c * GP:c * GP + G], gw_sb[:, c * P:(c + 1) * P],
                                             ident[0:G, 0:G])
                mm.then_inc(gw_tr, 1)

            def rows_transposes(g):
                pe.wait_ge(xn2_done, g + 1)
                pe.wait_ge(h2_done, g)
                pe.wait_ge(combT_done, 1)
                pe.wait_ge(vals_done, UNITS)
                if g > 1:
                    pe.wait_ge(y_done, B)
                for c in range(DC):
                    for t in range(TPT):
                        mm = nc.tensor.transpose(bank[rows_banks[g][c]][:, t * P:(t + 1) * P],
                                                 xn2[:, t, c * P:(c + 1) * P], ident[:])
                mm.then_inc(xn2_tr, 1)

            def half_transposes(c):
                if c == 0:
                    pe.wait_ge(xn2_done, 1)
                    pe.wait_ge(gw_done, 2)
                else:
                    pe.wait_ge(half_h2, 1)
                for t in range(TPT):
                    mm = nc.tensor.transpose(bank[rows_banks[0][c]][:, t * P:(t + 1) * P],
                                             xn2[:, t, c * P:(c + 1) * P], ident[:])
                mm.then_inc(xn2_tr if c else half_tr, 1)

            def logits(g):
                pe.wait_ge(h2_lo_done, g + 1)
                if g:
                    pe.wait_ge(x1_done, B)
                    pe.wait_ge(lgT_done, g)
                hi, low = rows_parts(g)
                three(bank[7][0:GP, :], [(gw_hi[:, c, :], gw_lo[:, c, :]) for c in range(DC)],
                      [(hi[:, c, :], low[:, c, :]) for c in range(DC)], True, True).then_inc(lgT_made, 1)

            def logit_transposes(w):
                pe.wait_ge(lgT_done, TILES if w else 1)
                pe.wait_ge(x1_done, B if w else B - 1)
                for t in range(experts[w].n):
                    src = logitsT[:, (TPT + t) * P:(TPT + t + 1) * P] if w else logitsT0[:, t * P:(t + 1) * P]
                    mm = nc.tensor.transpose(bank[7][:, t * GP:(t + 1) * GP], src, ident[0:GP, 0:GP])
                mm.then_inc(lg_made, 1)

            def comb_transposes(w):
                pe.wait_ge(comb_done, w + 1)
                for t in range(experts[w].n):
                    ps = bank[comb_banks[w][t // TPT]]
                    mm = nc.tensor.transpose(ps[0:2 * G, (t % TPT) * P:(t % TPT + 1) * P],
                                             experts[w].comb2[:, t, :], ident[:])
                mm.then_inc(comb_tr, 1)

            def spread_weights(t, j):
                f = slice(j * P, j * P + rows_of[j])
                weights = combT0[:] if isinstance(t, int) else combT[:, bass.ds(t * NT, NT)]
                nc.tensor.matmul(bank[2][0:rows_of[j], :], spread[:, f], weights,
                                 start=True, stop=True).then_inc(c_made, 1)

            def features(t, j, first):
                i = t * FT + j
                n = rows_of[j]
                f = slice(j * P, j * P + n)
                hi, low = rows_parts(t)
                rhs = [(hi[:, c, :], low[:, c, :]) for c in range(DC)]
                if first:
                    pe.wait_ge(gu_lo_done, j + 1)
                if first and j == 0:
                    pe.wait_ge(h2_lo_done, 1)
                    pe.wait_ge(qk_lo_done, UNITS)
                if not first or i:
                    pe.wait_ge(silu_done, i)
                three(bank[0][0:n, :], [(g_hi[:, c, f], g_lo[:, c, f]) for c in range(DC)], rhs,
                      True, True).then_inc(g_made, 1)
                if not first or i:
                    pe.wait_ge(fu_done, i)
                if not first or i:
                    pe.wait_ge(fc_done, i)
                three(bank[1][0:n, :], [(u_hi[:, c, f], u_lo[:, c, f]) for c in range(DC)], rhs,
                      True, True).then_inc(u_made, 1)
                if first and j == 0:
                    pe.wait_ge(combT_done, 1)
                    pe.wait_ge(spread_done, 1)
                    pe.wait_ge(exp_done, UNITS)
                elif j == 0:
                    pe.wait_ge(combT_done, 2)
                spread_weights(t, j)

            def down(t, j, first, i):
                n = rows_of[j]
                if first or j == FT - 1:
                    pe.wait_ge(d_lo_done, j + 1)
                pe.wait_ge(f_lo_done, i + 1)
                if j == 0 and isinstance(t, int) and t == 0:
                    pe.wait_ge(vals_done, UNITS)
                elif j == 0:
                    pe.wait_ge(y2_done, t)
                for c in range(DC):
                    q = slice(c * P, (c + 1) * P)
                    mm = three(acc2[c][:], [(d_hi[0:n, j, q], d_lo[0:n, j, q])],
                               [(f_hi[0:n, j % 2, :], f_lo[0:n, j % 2, :])], j == 0, j == FT - 1, skip=True)
                mm.then_inc(d_made, 1)

            def out_transposes(t):
                pe.wait_ge(y2_done, t + 1)
                if not (isinstance(t, int) and t == 0):
                    pe.wait_ge(x2_done, t)
                for k in range(TPT):
                    for c in range(DC):
                        mm = nc.tensor.transpose((tra, trb)[k // 2][:, k % 2, c * P:(c + 1) * P],
                                                 y2T[:, c, k * P:(k + 1) * P], ident[:])
                mm.then_inc(y2_tr, 1)

            for h in range(NH):
                step(B - 1, h)
                if h == GATE_STEP:
                    gate_weights()
                if h in ROWS_STEPS:
                    half_transposes(ROWS_STEPS.index(h))
                if h == LOGITS_STEP:
                    logits(0)
                if h == LOGITS_TR_STEP:
                    logit_transposes(0)
            for k in range(FFN_STEP + FT):
                if k == FFN_STEP:
                    features(0, 0, True)
                if k <= LAG["wo"]:
                    step(B, k)
                if k == COMB_STEP:
                    comb_transposes(0)
                j = k - FFN_STEP
                if j >= 0:
                    if j:
                        features(0, j, True)
                    at(j, logits, 3)
                    if j:
                        down(0, j - 1, True, j - 1)
                    if j == CHOICE_AT:
                        logit_transposes(1)
                    at(j, rows_transposes)
                if k == LAST_YT:
                    y_transposes(B - 1)
            comb_transposes(1)
            with pe.Fori(1, TILES) as t:
                for j in range(FT):
                    features(t, j, False)
                    if j == 0:
                        down(t - 1, FT - 1, False, t * FT - 1)
                    else:
                        down(t, j - 1, False, t * FT + j - 1)
                    if j == 2:
                        out_transposes(t - 1)
            down(TILES - 1, FT - 1, False, TILES * FT - 1)
            out_transposes(TILES - 1)


        @block.scalar
        def _(act):
            act.wait_ge(c_tr, 1)
            nc.scalar.activation(cTs, bank[0][:, 0:DC * B].rearrange("p (c b) -> p c b", c=DC),
                                 ACT.Silu).then_inc(c_silu, 1)

            def copy(dst, src):
                return nc.scalar.activation(dst, src, ACT.Copy)

            def split_head(h):
                act.wait_ge(w_in[h % SLOTS], 64 * (h // SLOTS + 1))
                raw = wraw[:, h % SLOTS, :]
                copy(wq_hi[:, h].rearrange("p a c d -> p (a c d)"), raw[:, 0:3 * D])
                copy(wo_hi[:, h, :], raw[:, 3 * D:4 * D]).then_inc(w_hi_done, 1)

            def split_qk(b, g, u):
                act.wait_ge(qk_made, u + 1)
                wait(act, s_made, u - 1)
                copy(qk_hi[:, g % 2], qk_ps[g % 2]).then_inc(qk_hi_done, 1)

            def exponentials(b, g, u):
                r = g % 2
                wait(act, psum_done, u - 1)
                act.wait_ge(nmax_done, u + 1)
                for t in range(TT):
                    e = nc.scalar.activation(probs[:, r, t, :], s_ps[r][:, t, :], ACT.Exp,
                                             bias=nmax[:, r, t:t + 1], scale=SCALE,
                                             accum_out=rsum[:, r, t:t + 1])
                e.then_inc(exp_done, 1)

            def split_psum(b, g, u):
                wait(act, v_made, u - 1)
                act.wait_ge(psum_done, u + 1)
                copy(psum_hi[:, g % 2, :], psum[:, g % 2, :]).then_inc(psum_hi_done, 1)

            def query_sums(b, g, u):
                wait(act, vals_done, u - 1)
                act.wait_ge(v_made, u + 1)
                copy(qsum[:, g % 2, :], v_ps[g % 2][:, 1, :]).then_inc(qsum_done, 1)

            def split_values(b, g, u):
                wait(act, wo_done, u - 1)
                act.wait_ge(vals_done, u + 1)
                copy(o_hi[:, g % 2, :], vals[:, g % 2, :]).then_inc(o_hi_done, 1)

            def step(b, h):
                turn(b, h, LAG["qsum"], query_sums)
                turn(b, h, LAG["split"], split_values)
                turn(b, h, LAG["exp"], exponentials)
                turn(b, h, 0, split_qk)
                turn(b, h, LAG["qsum_p"], split_psum)
                if isinstance(b, int) and b == 0 and h + 3 < NH:
                    split_head(h + 3)

            split_head(0)
            split_head(1)
            split_head(2)
            for h in range(NH):
                step(0, h)
            with act.Fori(1, B - 1) as b:
                for h in range(NH):
                    step(b, h)
            def split_down(j):
                n = rows_of[j]
                if j == 0:
                    act.wait_ge(dw_in, 48)
                copy(d_hi[0:n, j, :], draw[0:n, j, :]).then_inc(d_hi_done, 1)

            def split_features(j):
                f = slice(j * P, j * P + rows_of[j])
                if j == 0:
                    act.wait_ge(fw_in, 96)
                copy(g_hi[:, :, f], graw[:, :, f])
                copy(u_hi[:, :, f], uraw[:, :, f]).then_inc(gu_hi_done, 1)

            def modulate_rows(g, c):
                for k in range(BPT):
                    b, q = g * BPT + k, slice(k * S, (k + 1) * S)
                    m = nc.scalar.activation(h2[:, c, q], bank[rows_banks[g][c]][:, q], ACT.Identity,
                                             bias=mod[:, SB, c, b:b + 1], scale=mod[:, CB, c, b:b + 1])
                return m

            def modulate_half(c):
                act.wait_ge(xn2_tr if c else half_tr, 1)
                act.wait_ge(mod_ready, 1)
                modulate_rows(0, c).then_inc(h2_done if c else half_h2, 1)

            def modulate2(g):
                act.wait_ge(xn2_tr, g + 1)
                act.wait_ge(h2_lo_done, g)
                for c in range(DC):
                    m = modulate_rows(g, c)
                m.then_inc(h2_done, 1)

            def rows2_hi(g):
                act.wait_ge(h2_done, g + 1)
                if g == 1:
                    act.wait_ge(wo_done, UNITS)
                copy(rows_parts(g)[0][:], h2[:]).then_inc(h2_hi_done, 1)

            def logits_out(g):
                act.wait_ge(lgT_made, g + 1)
                copy(logitsT[:, g * NT:(g + 1) * NT] if g else logitsT0[:], bank[7][0:GP, :]).then_inc(lgT_done, 1)

            def gates_exp(w):
                act.wait_ge(gate_sub, w + 1)
                exps = experts[w].exps
                nc.scalar.activation(exps, exps, ACT.Exp).then_inc(gate_exp, 1)

            def comb_out(w):
                act.wait_ge(comb_tr, w + 1)
                for k, i in enumerate(comb_banks[w]):
                    m = copy(combT[:, (w + k) * NT:(w + k + 1) * NT] if w else combT0[:], bank[i][0:2 * G, 0:NT])
                m.then_inc(combT_done, 1)

            def product_hi(i, j, first):
                n = rows_of[j]
                act.wait_ge(fc_done, i + 1)
                if not first or i >= 2:
                    act.wait_ge(d_made, i - 1)
                r = j % 2
                copy(f_hi[0:n, j % 2, :], fu[0:n, r, :]).then_inc(f_hi_done, 1)

            def silu(i, j, first):
                n = rows_of[j]
                act.wait_ge(g_made, i + 1)
                if not first or i:
                    act.wait_ge(fu_done, i)
                nc.scalar.activation(fs[0:n, :], bank[0][0:n, :], ACT.Silu).then_inc(silu_done, 1)

            for h in range(NH):
                step(B - 1, h)
                if h - 1 in ROWS_STEPS:
                    modulate_half(ROWS_STEPS.index(h - 1))
                if h == LOGITS_STEP:
                    logits_out(0)
                if h == LOGITS_TR_STEP + 1:
                    gates_exp(0)
            for k in range(FFN_STEP + FT):
                if k < LAG["wo"]:
                    step(B, k)
                if k == COMB_STEP:
                    split_features(0)
                    comb_out(0)
                if k == SPREAD_STEP:
                    split_features(1)
                    act.wait_ge(spread_in_done, 16)
                    copy(spread[:], spread_raw[:]).then_inc(spread_done, 1)
                if k == FFN_STEP:
                    act.wait_ge(v_made, UNITS)
                    silu(0, 0, True)
                    split_down(0)
                    split_down(1)
                    split_features(2)
                j = k - FFN_STEP
                if j >= 0:
                    if j:
                        product_hi(j - 1, j - 1, True)
                        silu(j, j, True)
                    at(j, modulate2, 1)
                    at(j, rows2_hi, 2)
                    if j + 2 < FT:
                        split_down(j + 2)
                    if j + 3 < FT:
                        split_features(j + 3)
                    at(j, logits_out, 3)
                    if j == CHOICE_AT:
                        gates_exp(1)
            comb_out(1)
            with act.Fori(1, TILES) as t:
                for j in range(FT):
                    i = t * FT + j
                    product_hi(i - 1, (j - 1) % FT, False)
                    silu(i, j, False)
            product_hi(TILES * FT - 1, FT - 1, False)

        @block.vector
        def _(dve):
            def lo(dst, src, hi):
                return nc.vector.tensor_tensor(dst, src, f32(hi), ALU.subtract)

            chains = {}

            def link(s, ins):
                chains[s.name] = chains.get(s.name, 0) + 1
                ins.then_inc(s, 1)
                dve.wait_ge(s, chains[s.name])

            def deviation(n, v, y, t):
                ts, stt = nc.vector.tensor_scalar, nc.vector.scalar_tensor_tensor
                if n == 0:
                    return ts(v, v, LN_EPS, None, ALU.add)
                if n == 1:
                    return ts(t.bitcast(I32), v.bitcast(I32), 1, None, ALU.arith_shift_right)
                if n == 2:
                    return ts(y.bitcast(I32), t.bitcast(I32), -1.0, float(0x5F3759DF), ALU.mult, ALU.add)
                if n % 3 == 0:
                    return stt(t, y, -0.5, y, ALU.mult, ALU.mult)
                if n % 3 == 1:
                    return nc.vector.tensor_tensor(t, t, v, ALU.mult)
                return stt(y, t, 1.5, y, ALU.add, ALU.mult)


            GATE_PARTS = 5

            def gate(k, src, n):
                sgn, mag = mtmp[:, 0], mtmp[:, 1]
                dve.wait_ge(mod_chain, chains[mod_chain.name])
                chains[mod_chain.name] += 1
                if n == 0:
                    m = nc.vector.tensor_scalar(sgn, src, 0.0, 2.0, ALU.is_ge, ALU.mult)
                elif n == 1:
                    m = nc.vector.tensor_scalar(sgn, sgn, -1.0, None, ALU.add)
                elif n == 2:
                    m = nc.vector.tensor_tensor(mag, sgn, src, ALU.mult)
                elif n == 3:
                    m = nc.vector.tensor_scalar(mag, mag, GATE_MIN, None, ALU.max)
                else:
                    m = nc.vector.tensor_tensor(mod[:, k, :, 0:B], sgn, mag, ALU.mult)
                m.then_inc(mod_chain, 1)

            def normalise(b, n):
                if n:
                    dve.wait_ge(ln_chain, LN_LINKS * b + n)
                if n == 0:
                    dve.wait_ge(x_in, 16 * (b + 1))
                    for t in range(TT):
                        st = nc.vector.bn_stats(stats[:, t, :], x_ln[:, t, :])
                    st.then_inc(ln_chain, 1)
                elif n == 1:
                    nc.vector.memset(rtmp[:], 0.0)
                    for t in range(TT):
                        st = nc.vector.bn_aggr(mv[:, t, :], stats[:, t, :])
                    st.then_inc(ln_chain, 1)
                elif n < LN_LINKS:
                    deviation(n - 2, mv[:, :, 1], rstd[:], rtmp[:]).then_inc(ln_chain, 1)
                else:
                    if not isinstance(b, int) or b:
                        dve.wait_ge(xn_tr, b)
                    for t in range(TT):
                        st = nc.vector.tensor_scalar(xn[:, t, :], x_ln[:, t, :], mv[:, t, 0:1],
                                                     rstd[:, t:t + 1], ALU.subtract, ALU.mult)
                    st.then_inc(xn_done, 1)

            def modulate(b):
                dve.wait_ge(xn_tr, b + 1)
                wait(dve, h_lo_done, b)
                for c in range(DC):
                    m = nc.vector.tensor_scalar(h_next[:, c, :], tr[:, c, :], mod[:, CA, c, bass.ds(b, 1)],
                                                mod[:, SA, c, bass.ds(b, 1)], ALU.mult, ALU.add)
                m.then_inc(hn_done, 1)

            def split_activations(b):
                q = bass.ds((b % 2) * S, S)
                dve.wait_ge(hn_done, b + 1)
                if not isinstance(b, int) or b >= 2:
                    dve.wait_ge(v_made, (b - 1) * NH)
                nc.vector.tensor_scalar(h_hi[:, :, q], h_next[:], 1.0, None, ALU.mult).then_inc(h_hi_done, 1)
                dve.wait_ge(h_hi_done, b + 1)
                lo(h_lo[:, :, q], h_next[:], h_hi[:, :, q]).then_inc(h_lo_done, 1)

            for n in range(LN_LINKS + 1):
                normalise(0, n)
            dve.wait_ge(mod_made, 1)
            mps = bank[1][:, 0:MODS * B].rearrange("p (k c b) -> p k c b", k=6, c=DC)
            link(mod_chain, nc.vector.tensor_copy(mod[:, SA, :, 0:B], mps[:, SA]))
            link(mod_chain, nc.vector.tensor_scalar(mod[:, CA, :, 0:B], mps[:, CA], 1.0, None, ALU.add))
            modulate(0)
            split_activations(0)
            nc.vector.tensor_scalar(ones[:], ident[:], 0.0, 1.0, ALU.mult, ALU.add).then_inc(ones_done, 1)
            def split_qk(b, g, u):
                dve.wait_ge(qk_hi_done, u + 1)
                lo(qk_lo[:, g % 2], qk_ps[g % 2], qk_hi[:, g % 2]).then_inc(qk_lo_done, 1)

            def row_max(b, g, u):
                r = g % 2
                dve.wait_ge(s_made, u + 1)
                nc.vector.tensor_reduce(smax[:, r, :], s_ps[r], AX_X, ALU.max).then_inc(smax_done, 1)
                dve.wait_ge(smax_done, u + 1)
                nc.vector.tensor_scalar(nmax[:, r, :], smax[:, r, :], -SCALE, None, ALU.mult).then_inc(nmax_done, 1)

            def row_inverse(b, g, u):
                dve.wait_ge(exp_done, u + 1)
                nc.vector.reciprocal(rinv[:, g % 2, :], rsum[:, g % 2, :]).then_inc(rinv_done, 1)

            def half_sum(b, g, u):
                r = g % 2
                dve.wait_ge(rinv_done, u + 1)
                nc.vector.tensor_scalar(psum_half[:, r, :], probs[:, r, 0, :], rinv[:, r, 0:1], None,
                                        ALU.mult).then_inc(half_done, 1)

            def full_sum(b, g, u):
                r = g % 2
                wait(dve, psum_lo_done, u - 1)
                dve.wait_ge(half_done, u + 1)
                nc.vector.scalar_tensor_tensor(psum[:, r, :], probs[:, r, 1, :], rinv[:, r, 1:2],
                                               psum_half[:, r, :], ALU.mult, ALU.add).then_inc(psum_done, 1)

            def times_v(b, g, u):
                r = g % 2
                wait(dve, o_lo_done, u - 1)
                dve.wait_ge(qsum_done, u + 1)
                nc.vector.tensor_tensor(vals[:, r, :], v_ps[r][:, 0, :], qsum[:, r, :],
                                        ALU.mult).then_inc(vals_done, 1)

            def gated_output(b):
                dve.wait_ge(wo_done, (b + 1) * NH)
                wait(dve, y_tr, b)
                for c in range(DC):
                    m = nc.vector.tensor_scalar(yT[:, c, :], acc[:, c, :], mod[:, GA, c, bass.ds(b, 1)],
                                                None, ALU.mult)
                m.then_inc(y_done, 1)

            def residual1(b):
                dve.wait_ge(y_tr, b + 1)
                dve.wait_ge(xres_in, 16 * (b + 1))
                nc.vector.tensor_tensor(x1[:, bass.ds(TT * b, TT), :], x_res[:], tr, ALU.add).then_inc(x1_done, 1)

            def other_modulations(n):
                mps2 = bank[7][:, 0:MODS * B].rearrange("p (k c b) -> p k c b", k=6, c=DC)
                if n == 0:
                    dve.wait_ge(mod_made, MOD_STEP)
                    nc.vector.tensor_copy(mod[:, SB, :, 0:B], mps2[:, SB])
                    nc.vector.tensor_scalar(mod[:, CB, :, 0:B], mps2[:, CB], 1.0, None, ALU.add)
                elif n <= GATE_PARTS:
                    gate(GA, mps2[:, GA], n - 1)
                else:
                    gate(GB, mps2[:, GB], n - 1 - GATE_PARTS)
                if n == 2 * GATE_PARTS:
                    dve.wait_ge(mod_chain, chains[mod_chain.name])
                    nc.vector.memset(mtmp[:, 0, 0, 0:1], 0.0).then_inc(mod_ready, 1)

            def output_weights_lo(h):
                dve.wait_ge(w_hi_done, h + 1)
                lo(wo_lo[:, h, :], wraw[:, h % SLOTS, 3 * D:4 * D], wo_hi[:, h, :]).then_inc(wo_lo_done, 1)

            output_weights_lo(0)
            output_weights_lo(1)

            def step(b, h):
                last = isinstance(b, int) and b == B
                peeled = isinstance(b, int) and b == B - 1
                some = not (isinstance(b, int) and b == 0)
                if some and h == STEP_Y:
                    gated_output(b - 1)

                def then_part(k):
                    n = (h - MOD_STEP) * STAGES + k
                    if not some and 0 <= n <= 2 * GATE_PARTS:
                        other_modulations(n)
                    n = (h - STEP_LN) * STAGES + k
                    if not last and not peeled and 0 <= n <= LN_LINKS:
                        normalise(b + 1, n)
                    n = (h - LN2_STEP) * STAGES + k
                    if peeled and 0 <= n <= LN_LINKS:
                        normalise2(0, n)

                turn(b, h, LAG["qsum_p"], row_inverse)
                then_part(0)
                turn(b, h, LAG["vals"], times_v)
                then_part(1)
                turn(b, h, LAG["qsum_p"], half_sum)
                then_part(2)
                turn(b, h, LAG["qsum_p"], full_sum)
                then_part(3)
                turn(b, h, LAG["smax"], row_max)
                then_part(4)
                turn(b, h, 0, split_qk)
                then_part(5)
                if not some and h + 2 < NH:
                    output_weights_lo(h + 2)
                if some and h == STEP_X1:
                    residual1(b - 1)
                if not last and not peeled and h == STEP_HN:
                    modulate(b + 1)
                if not last and not peeled and h == STEP_HN + 1:
                    split_activations(b + 1)

            def normalise2(g, n):
                rows = x1[:, g * TPT:(g + 1) * TPT, :]
                small = ln2_small[min(g, 1)]
                stats2, mv2, rstd2, rtmp2 = small[:, :, 0:6], small[:, :, 6:8], small[:, :, 8], small[:, :, 9]
                if n:
                    dve.wait_ge(ln2_chain, LN_LINKS * g + n)
                if n == 0:
                    dve.wait_ge(x1_done, BPT * (g + 1))
                    for t in range(TPT):
                        st = nc.vector.bn_stats(stats2[:, t, :], rows[:, t, :])
                    st.then_inc(ln2_chain, 1)
                elif n == 1:
                    for t in range(TPT):
                        st = nc.vector.bn_aggr(mv2[:, t, :], stats2[:, t, :])
                    st.then_inc(ln2_chain, 1)
                elif n < LN_LINKS:
                    deviation(n - 2, mv2[:, :, 1], rstd2, rtmp2).then_inc(ln2_chain, 1)
                else:
                    if g:
                        dve.wait_ge(xn2_tr, g)
                    for t in range(TPT):
                        st = nc.vector.tensor_scalar(xn2[:, t, :], rows[:, t, :], mv2[:, t, 0:1],
                                                     rstd2[:, t:t + 1], ALU.subtract, ALU.mult)
                    st.then_inc(xn2_done, 1)

            def split_half(c):
                dve.wait_ge(h2_done if c else half_h2, 1)
                nc.vector.tensor_copy(h2_hi0[:, c, :], h2[:, c, :]).then_inc(half_hi, 1)
                dve.wait_ge(half_hi, c + 1)
                m = lo(h2_lo0[:, c, :], h2[:, c, :], h2_hi0[:, c, :])
                if c == DC - 1:
                    m.then_inc(h2_lo_done, 1)

            def choose(w, part):
                x = experts[w]
                n, pr = x.n, x.probs
                tt, ts, red = nc.vector.tensor_tensor, nc.vector.tensor_scalar, nc.vector.tensor_reduce

                def wide(ap):
                    return ap.unsqueeze(2).to_broadcast([P, n, E])

                def largest(src, m, sel):
                    link(gate_chain, red(m, src, AX_X, ALU.max))
                    link(gate_chain, tt(sel, src, wide(m), ALU.is_equal))
                    link(gate_chain, tt(sel, sel, order.to_broadcast([P, n, E]), ALU.mult))
                    link(gate_chain, red(x.rank, sel, AX_X, ALU.max))
                    link(gate_chain, tt(sel, sel, wide(x.rank), ALU.is_equal))

                if part == 0:
                    dve.wait_ge(lg_made, w + 1)
                    logit = bank[7][:, 0:n * GP].rearrange("p (t e) -> p t e", t=n)
                    link(gate_chain, red(x.m1, logit[:, :, 0:E], AX_X, ALU.max))
                    link(gate_chain, tt(x.exps[:, :, 0:E], logit[:, :, 0:E], wide(x.m1), ALU.subtract))
                    ts(x.exps[:, :, E:G], logit[:, :, E:G], -1.0, None, ALU.mult).then_inc(gate_sub, 1)
                elif part == 1:
                    dve.wait_ge(gate_exp, w + 1)
                    link(gate_chain, red(x.total, x.exps[:, :, 0:E], AX_X, ALU.add))
                    link(gate_chain, nc.vector.reciprocal(x.total, x.total))
                    link(gate_chain, tt(pr, x.exps[:, :, 0:E], wide(x.total), ALU.mult))
                elif part == 2:
                    dve.wait_ge(rank_in, 16)
                    largest(pr, x.m1, x.sel1)
                    link(gate_chain, nc.vector.scalar_tensor_tensor(x.masked, x.sel1, -2.0, pr, ALU.mult, ALU.add))
                elif part == 3:
                    largest(x.masked, x.m2, x.sel2)
                elif part == 4:
                    tt(x.total, x.m1, x.m2, ALU.add)
                    ts(x.rank, x.exps[:, :, E], 1.0, None, ALU.add)
                    link(gate_chain, tt(x.sel1, x.sel1, x.sel2, ALU.add))
                    nc.vector.reciprocal(x.total, x.total)
                    nc.vector.reciprocal(x.comb[:, :, E], x.rank)
                    link(gate_chain, tt(x.sel1, x.sel1, pr, ALU.mult))
                    link(gate_chain, tt(x.comb[:, :, 0:E], x.sel1, wide(x.total), ALU.mult))
                else:
                    link(gate_chain, nc.vector.tensor_copy(x.comb_r, x.comb))
                    nc.vector.tensor_copy(x.comb2[:, :, 0:G], f32(x.comb_r))
                    link(gate_chain, tt(x.comb, x.comb, f32(x.comb_r), ALU.subtract))
                    nc.vector.tensor_copy(x.comb2[:, :, G:2 * G], x.comb).then_inc(comb_done, 1)

            def gate_weights():
                dve.wait_ge(gw_tr, 1)
                gps = bank[7][:, 0:DC * GP].rearrange("p (c g) -> p c g", c=DC)
                link(gate_chain, nc.vector.memset(gwT, 0.0))
                link(gate_chain, nc.vector.tensor_copy(gwT[:, :, 0:G], gps[:, :, 0:G]))
                nc.vector.tensor_copy(gw_hi, gwT).then_inc(gw_done, 1)
                dve.wait_ge(gw_done, 1)
                lo(gw_lo, gwT, gw_hi).then_inc(gw_done, 1)

            STAGES = 6
            for h in range(NH):
                step(0, h)
            with dve.Fori(1, B - 1) as b:
                for h in range(NH):
                    step(b, h)
            for h in range(NH):
                step(B - 1, h)
                if h == GATE_STEP + 1:
                    gate_weights()
                if h - 2 in ROWS_STEPS:
                    split_half(ROWS_STEPS.index(h - 2))
                for part in CHOICE_STEPS.get((B - 1, h), ()):
                    choose(0, part)

            def product_lo(i, j):
                n = rows_of[j]
                dve.wait_ge(f_hi_done, i + 1)
                r = j % 2
                lo(f_lo[0:n, j % 2, :], fu[0:n, r, :], f_hi[0:n, j % 2, :]).then_inc(f_lo_done, 1)

            def product(i, j, first):
                n = rows_of[j]
                r = j % 2
                if not first or i >= 2:
                    dve.wait_ge(f_lo_done, i - 1)
                dve.wait_ge(silu_done, i + 1)
                dve.wait_ge(u_made, i + 1)
                nc.vector.tensor_tensor(fu[0:n, r, :], fs[0:n, :], bank[1][0:n, :], ALU.mult).then_inc(fu_done, 1)
                dve.wait_ge(fu_done, i + 1)
                dve.wait_ge(c_made, i + 1)
                nc.vector.tensor_tensor(fu[0:n, r, :], fu[0:n, r, :], bank[2][0:n, :], ALU.mult).then_inc(fc_done, 1)

            def scaled_output(t):
                dve.wait_ge(d_made, (t + 1) * FT)
                if not (isinstance(t, int) and t == 0):
                    dve.wait_ge(y2_tr, t)
                for c in range(DC):
                    for k in range(BPT):
                        q = slice(k * S, (k + 1) * S)
                        m = nc.vector.tensor_scalar(y2T[:, c, q], bank[3 + c][:, q],
                                                    mod[:, GB, c, bass.ds(BPT * t + k, 1)], None, ALU.mult)
                m.then_inc(y2_done, 1)

            def residual(t):
                dve.wait_ge(y2_tr, t + 1)
                if not (isinstance(t, int) and t == 0):
                    dve.wait_ge(out_done, 16 * t)
                for k in range(2):
                    src = bank[5 + k][:].rearrange("p (c s) -> p c s", c=2)
                    m = nc.vector.tensor_tensor(x2[:, 2 * k:2 * k + 2, :], x1[:, bass.ds(t * TPT + 2 * k, 2), :],
                                                src, ALU.add)
                m.then_inc(x2_done, 1)

            for k in range(FFN_STEP + FT):
                if k < STEP_Y:
                    step(B, k)
                for part in CHOICE_STEPS.get((B, k), ()):
                    choose(0, part)
                j = k - FFN_STEP
                if j >= 0:
                    if j:
                        product_lo(j - 1, j - 1)
                    if 0 < j - CHOICE_AT < 4:
                        choose(1, 2 * (j - CHOICE_AT) - 1)
                    if k == STEP_Y:
                        gated_output(B - 1)
                    if k == LAST_X1:
                        residual1(B - 1)
                    product(j, j, True)
                    for g, n in NORM_AT.get(j, ()):
                        normalise2(g, n)
                    if 0 <= j - CHOICE_AT < 3:
                        choose(1, 2 * (j - CHOICE_AT))
            with dve.Fori(1, TILES) as t:
                for j in range(FT):
                    i = t * FT + j
                    product_lo(i - 1, (j - 1) % FT)
                    product(i, j, False)
                    if j == 0:
                        scaled_output(t - 1)
                    if j == 2:
                        residual(t - 1)
            product_lo(TILES * FT - 1, FT - 1)
            scaled_output(TILES - 1)
            residual(TILES - 1)

        @block.gpsimd
        def _(pool):
            def split_head(h):
                pool.wait_ge(w_hi_done, h + 1)
                raw = wraw[:, h % SLOTS, :]
                nc.gpsimd.tensor_tensor(wq_lo[:, h].rearrange("p a c d -> p (a c d)"), raw[:, 0:3 * D],
                                        f32(wq_hi[:, h].rearrange("p a c d -> p (a c d)")),
                                        ALU.subtract).then_inc(w_lo_done, 1)

            def split_psum(b, g, u):
                r = g % 2
                pool.wait_ge(psum_hi_done, u + 1)
                nc.gpsimd.tensor_tensor(psum_lo[:, r, :], psum[:, r, :], f32(psum_hi[:, r, :]),
                                        ALU.subtract).then_inc(psum_lo_done, 1)

            def split_values(b, g, u):
                r = g % 2
                pool.wait_ge(o_hi_done, u + 1)
                nc.gpsimd.tensor_tensor(o_lo[:, r, :], vals[:, r, :], f32(o_hi[:, r, :]),
                                        ALU.subtract).then_inc(o_lo_done, 1)

            def step(b, h):
                turn(b, h, LAG["split"], split_values)
                turn(b, h, LAG["qsum_p"], split_psum)

            for h in range(3):
                split_head(h)
            for h in range(NH):
                step(0, h)
                if h + 3 < NH:
                    split_head(h + 3)
            with pool.Fori(1, B - 1) as b:
                for h in range(NH):
                    step(b, h)
            for h in range(NH):
                step(B - 1, h)

            def split_features(j):
                f = slice(j * P, j * P + rows_of[j])
                pool.wait_ge(gu_hi_done, j + 1)
                nc.gpsimd.tensor_tensor(g_lo[:, :, f], graw[:, :, f], f32(g_hi[:, :, f]), ALU.subtract)
                nc.gpsimd.tensor_tensor(u_lo[:, :, f], uraw[:, :, f], f32(u_hi[:, :, f]),
                                        ALU.subtract).then_inc(gu_lo_done, 1)

            def split_down(j):
                n = rows_of[j]
                pool.wait_ge(d_hi_done, j + 1)
                nc.gpsimd.tensor_tensor(d_lo[0:n, j, :], draw[0:n, j, :], f32(d_hi[0:n, j, :]),
                                        ALU.subtract).then_inc(d_lo_done, 1)

            def rows2_lo(g):
                pool.wait_ge(h2_hi_done, g)
                hi, low = rows_parts(g)
                nc.gpsimd.tensor_tensor(low[:], h2[:], f32(hi[:]), ALU.subtract).then_inc(h2_lo_done, 1)

            for k in range(FT + FFN_STEP):
                if k < LAG["split"]:
                    step(B, k)
                j = k - FFN_STEP
                if j == 0:
                    split_down(0)
                if 0 <= j and j + 1 < FT:
                    split_down(j + 1)
                if 0 <= j + 2 < FT:
                    split_features(j + 2)
                at(j, rows2_lo, 2)


_INS = ["L0_attn_x", "L0_attn_w_qkv", "L0_attn_w_o", "L0_ffn_gate_w", "L0_ffn_w_gate", "L0_ffn_w_up",
        "L0_ffn_w_down", "L0_ffn_shgate_w", "L0_ffn_shw_gate", "L0_ffn_shw_up", "L0_ffn_shw_down",
        "L0_c", "L0_wmod"]


def kernel(**inputs):
    import numpy as np
    import concourse.bacc as bacc
    from concourse.bass_utils import run_bass_kernel_spmd

    arrays = {name: np.ascontiguousarray(inputs[name]) for name in _INS}
    experts, _, hidden = arrays["L0_ffn_w_gate"].shape
    features = experts * hidden + arrays["L0_ffn_shw_gate"].shape[1]
    spread = np.zeros((2, experts + 1, -(-features // P) * P), np.float32)
    for e in range(experts):
        spread[:, e, e * hidden:(e + 1) * hidden] = 1
    spread[:, experts, experts * hidden:features] = 1
    arrays["ident"] = np.eye(P, dtype=np.float32)
    arrays["spread"] = spread.reshape(2 * (experts + 1), -1)
    ranks = np.arange(experts, 0, -1, dtype=np.float32)
    arrays["order"] = np.tile(ranks, (P, 1))

    nc = bacc.Bacc("TRN2", target_bir_lowering=False, num_devices=1)
    args = [nc.dram_tensor(f"in_{n}", a.shape, mybir.dt.from_np(a.dtype), kind="ExternalInput").ap()
            for n, a in arrays.items()]
    out = nc.dram_tensor("out", arrays["L0_attn_x"].shape, F32, kind="ExternalOutput").ap()
    adaln_block(nc, *args, out)
    r = run_bass_kernel_spmd(nc, [{f"in_{n}": a for n, a in arrays.items()}], core_ids=[0])
    return r.results[0]["out"]
```
